# Optimizing a Trainium2 kernel written in Bass

```python
import numpy as np
import jax
import jax.numpy as jnp

def _softmax(x, axis=-1):
    return jax.nn.softmax(x, axis=axis)

def _gelu(x):
    return jax.nn.gelu(x, approximate=True)

def _silu(x):
    return jax.nn.silu(x)

def _sigmoid(x):
    return jax.nn.sigmoid(x)

def _layernorm(x, axis=-1, eps=1e-05):
    m = jnp.mean(x, axis=axis, keepdims=True)
    v = jnp.var(x, axis=axis, keepdims=True)
    return (x - m) / jnp.sqrt(v + eps)

def _scatter_add(tgt, idx, src, axis=0):
    return tgt.at[idx].add(src)

def _segment_sum(src, seg, n):
    return jax.ops.segment_sum(src, seg, n)
kernel_name = 'mk_cond_resid_d2_seqx_r4_0ec575'

def setup_inputs(seed: int=0):
    np.random.seed(seed)
    _w = jnp.asarray

    def _rec_inputs():
        import jax
        import jax.numpy as jnp
        _rk = jax.random.key(seed)
        x = -0.0003929 + 0.9999 * jax.random.normal(jax.random.fold_in(_rk, 1), (64, 64, 1024), jnp.float32)
        _lenS = 64 - jax.random.randint(jax.random.fold_in(_rk, 7), (64,), 0, max(1, 64 // 4) + 1, jnp.int32)
        _lenS2 = 64 - jax.random.randint(jax.random.fold_in(_rk, 8), (64,), 0, max(1, 64 // 4) + 1, jnp.int32)
        itok_B_8_3872 = jax.random.randint(jax.random.fold_in(_rk, 11), (64,), 8, 3873, jnp.int32)
        itok_B_0_7 = jax.random.randint(jax.random.fold_in(_rk, 12), (64,), 0, 8, jnp.int32)
        return (x, itok_B_8_3872, itok_B_0_7)
    x, itok_B_8_3872, itok_B_0_7 = _rec_inputs()

    def _L0_cond_setup():
        import math
        import jax, jax.numpy as jnp
        import numpy as np
        H, N, B, L = (64, 64, 16, 1024)
        DT_MIN, DT_MAX = (0.001, 0.1)

        def _get_kernel(log_dt, C, log_A_real, A_imag, length):
            Cc = C[..., 0] + 1j * C[..., 1]
            dt = jnp.exp(log_dt)
            A = -jnp.exp(log_A_real) + 1j * A_imag
            dtA = A * dt[:, None]
            P = dtA[:, :, None] * jnp.arange(length, dtype=jnp.float32)
            Cs = Cc * (jnp.exp(dtA) - 1.0) / A
            K = 2.0 * jnp.einsum('hn,hnl->hl', Cs, jnp.exp(P)).real
            return K
        key = jax.random.key(seed)
        ks = jax.random.split(key, 6)
        u = jax.random.normal(ks[0], (B, H, L), dtype=jnp.float32)
        length = jax.random.randint(ks[1], (B,), 0, L)
        log_dt = jax.random.uniform(ks[2], (H,), dtype=jnp.float32) * (math.log(DT_MAX) - math.log(DT_MIN)) + math.log(DT_MIN)
        C = jax.random.normal(ks[3], (H, N, 2), dtype=jnp.float32)
        log_A_real = jnp.log(0.5 * jnp.ones((H, N), dtype=jnp.float32))
        A_imag = math.pi * jnp.broadcast_to(jnp.arange(N, dtype=jnp.float32), (H, N))
        D = jax.random.normal(ks[4], (H,), dtype=jnp.float32)
        return {'u': u, 'length': length, 'log_dt': log_dt, 'C': C, 'log_A_real': log_A_real, 'A_imag': A_imag, 'D': D}
    _L0_cond_all = _L0_cond_setup()
    _L0_cond_in = {k: v for k, v in _L0_cond_all.items() if k in ('log_dt', 'C', 'log_A_real', 'A_imag', 'D')}
    del _L0_cond_all

    def _L1_cond_setup():
        import jax, jax.numpy as jnp
        import numpy as np
        TOP_K = 2
        LANG_BIAS = 5.0
        SCALING = 32.0 / 16.0
        LANGUAGE_PAD_ID = -1
        key = jax.random.key(seed)
        ks = jax.random.split(key, 6)
        B, T, D, O, E, R = (4, 512, 1024, 1024, 8, 16)
        x = jax.random.normal(ks[0], (B, T, D), dtype=jnp.float32)
        language_ids = jax.random.randint(ks[1], (B,), 0, E).astype(jnp.int64)
        W = jax.random.normal(ks[2], (O, D), dtype=jnp.float32) * (1.0 / np.sqrt(D))
        Wr = jax.random.normal(ks[3], (E, D), dtype=jnp.float32) * (1.0 / np.sqrt(D))
        A = jax.random.normal(ks[4], (E, R, D), dtype=jnp.float32) * (1.0 / np.sqrt(D))
        Bm = jax.random.normal(ks[5], (O, R), dtype=jnp.float32) * 0.0
        Bm = jnp.broadcast_to(Bm, (E, O, R)) + jax.random.normal(ks[5], (E, O, R), dtype=jnp.float32) * 0.02
        return {'x': x, 'language_ids': language_ids, 'W': W, 'Wr': Wr, 'A': A, 'B': Bm}
    _L1_cond_all = _L1_cond_setup()
    _L1_cond_in = {k: v for k, v in _L1_cond_all.items() if k in ('W', 'Wr', 'A', 'B')}
    del _L1_cond_all
    return {'x': x, 'itok_B_8_3872': itok_B_8_3872, 'itok_B_0_7': itok_B_0_7, 'L0_cond_log_dt': _L0_cond_in['log_dt'], 'L0_cond_C': _L0_cond_in['C'], 'L0_cond_log_A_real': _L0_cond_in['log_A_real'], 'L0_cond_A_imag': _L0_cond_in['A_imag'], 'L0_cond_D': _L0_cond_in['D'], 'L1_cond_W': _L1_cond_in['W'], 'L1_cond_Wr': _L1_cond_in['Wr'], 'L1_cond_A': _L1_cond_in['A'], 'L1_cond_B': _L1_cond_in['B']}

def reference(x, itok_B_8_3872, itok_B_0_7, L0_cond_log_dt, L0_cond_C, L0_cond_log_A_real, L0_cond_A_imag, L0_cond_D, L1_cond_W, L1_cond_Wr, L1_cond_A, L1_cond_B):
    import jax
    import jax.numpy as jnp

    def _L0_cond_ref(u, length, log_dt, C, log_A_real, A_imag, D):
        import math
        import jax, jax.numpy as jnp
        import numpy as np
        H, N, B, L = (64, 64, 16, 1024)
        DT_MIN, DT_MAX = (0.001, 0.1)

        def _get_kernel(log_dt, C, log_A_real, A_imag, length):
            Cc = C[..., 0] + 1j * C[..., 1]
            dt = jnp.exp(log_dt)
            A = -jnp.exp(log_A_real) + 1j * A_imag
            dtA = A * dt[:, None]
            P = dtA[:, :, None] * jnp.arange(length, dtype=jnp.float32)
            Cs = Cc * (jnp.exp(dtA) - 1.0) / A
            K = 2.0 * jnp.einsum('hn,hnl->hl', Cs, jnp.exp(P)).real
            return K
        Bq, Hq, Lq = u.shape
        mask = (jnp.arange(Lq) < length[:, None]).astype(u.dtype)
        u_m = u * mask[:, None, :]
        kernel = _get_kernel(log_dt, C, log_A_real, A_imag, Lq)
        n = 2 * Lq
        k_f = jnp.fft.rfft(kernel, n=n)
        u_f = jnp.fft.rfft(u_m, n=n)
        y = jnp.fft.irfft(u_f * k_f, n=n)[..., :Lq]
        y = y + u_m * D[:, None]
        return y * mask[:, None, :]

    def _L1_cond_ref(x, language_ids, W, Wr, A, B):
        import jax, jax.numpy as jnp
        import numpy as np
        TOP_K = 2
        LANG_BIAS = 5.0
        SCALING = 32.0 / 16.0
        LANGUAGE_PAD_ID = -1
        base = jnp.einsum('btd,od->bto', x, W)
        E = Wr.shape[0]
        logits = jnp.einsum('btd,ed->bte', x.astype(jnp.float32), Wr.astype(jnp.float32))
        expert_targets = language_ids
        valid = expert_targets >= 0
        tgt = jnp.where(valid, expert_targets, 0)
        bias = jax.nn.one_hot(tgt, E, dtype=logits.dtype) * LANG_BIAS
        bias = jnp.where(valid[:, None], bias, 0.0)
        logits = logits + bias[:, None, :]
        topw, topi = jax.lax.top_k(logits, TOP_K)
        weights = jax.nn.softmax(topw, axis=-1)
        gates = jnp.sum(jax.nn.one_hot(topi, E, dtype=weights.dtype) * weights[..., None], axis=-2)
        gates = gates.astype(x.dtype)
        h = jnp.einsum('btd,erd->bter', x, A)
        lora_out = jnp.einsum('bter,bte,eor->bto', h, gates, B)
        return base + SCALING * lora_out
    x = x + _L0_cond_ref(x, itok_B_8_3872, L0_cond_log_dt, L0_cond_C, L0_cond_log_A_real, L0_cond_A_imag, L0_cond_D)
    x = x + _L1_cond_ref(x, itok_B_0_7, L1_cond_W, L1_cond_Wr, L1_cond_A, L1_cond_B)
    return x

_drawn_inputs = setup_inputs


def setup_inputs(seed=0):
    import zlib

    import numpy as np

    out = dict(_drawn_inputs(seed))
    spreads = {'L0_cond_log_A_real': (-0.6931471824645996, 0.2)}
    factors = {}
    for name, (base, spread) in spreads.items():
        noise = np.random.default_rng([zlib.crc32(name.encode()), seed]).standard_normal(out[name].shape)
        drawn = base * np.exp(spread * noise) if base else spread * noise
        out[name] = jnp.asarray(drawn.astype(out[name].dtype))
    for name, factor in factors.items():
        out[name] = (out[name] * factor).astype(out[name].dtype)
    return out
```

```python
import math
from contextlib import ExitStack

import concourse.bass as bass
from concourse import mybir

F32 = mybir.dt.float32
F32R = mybir.dt.float32r
I32 = mybir.dt.int32
U32 = mybir.dt.uint32
ALU = mybir.AluOpType
ACT = mybir.ActivationFunctionType

P = 128
SEQS, HEADS, LEN = 64, 64, 1024
MODES = 64
CH = LEN // P
PAIRS = HEADS // 2
LEAD = 2
EXPERTS, RANK = 8, 16
ER = EXPERTS * RANK
LANG_BIAS, SCALING = 5.0, 2.0
WCOLS = LEN + ER + EXPERTS
BANKS = [(0, 388), (388, 776), (776, WCOLS)]
GATE = BANKS[2]
H0 = LEN - GATE[0]
L0 = H0 + ER
KPITCH = LEN + P

NA, NB = 16, 64
POS = NB + NA
KG = 8
KGROUPS = HEADS // KG
MAGIC = 1.5 * 2.0 ** 23
LN2_HI, LN2_LO = 0.693359375, -2.12194440054690583e-4
TWO_PI = 6.283185


def cond_resid_kernel(nc, x, lengths, languages, log_dt, C, log_A_real, A_imag, D, W, Wr, A, B, out):
    kpad = nc.dram_tensor("kpad", (HEADS, KPITCH), F32, kind="Internal").ap()
    with ExitStack() as ctx:
        def sb(name, shape, dt=F32):
            return ctx.enter_context(nc.sbuf_tensor(name, shape, dt))

        def pb(name, shape):
            return ctx.enter_context(nc.psum_tensor(name, shape, F32))

        def sem(name):
            return ctx.enter_context(nc.semaphore(name))

        w_hi = sb("w_hi", [P, CH, WCOLS], F32R)
        w_lo = sb("w_lo", [P, CH, WCOLS], F32R)
        bt_hi = sb("bt_hi", [P, LEN], F32R)
        bt_lo = sb("bt_lo", [P, LEN], F32R)
        valid = sb("valid", [P, CH, SEQS], I32)
        bias = sb("bias", [P, EXPERTS])
        ident = sb("ident", [P, P])
        expert_no = sb("expert_no", [P, EXPERTS])
        rows = [sb(f"rows{s}", [P, LEN]) for s in range(2)]
        xt = [sb(f"xt{s}", [P, CH, P]) for s in range(2)]
        u_hi = [sb(f"u_hi{s}", [P, LEAD + CH, P], F32R) for s in range(2)]
        u_lo = [sb(f"u_lo{s}", [P, LEAD + CH, P], F32R) for s in range(2)]
        toe = [sb(f"toe{s}", [P, 2, LEN]) for s in range(2)]
        toe_f = [bass.AP(t[:, :, :].tensor, LEN - 1, [[2 * LEN, P], [LEN, 2], [-1, LEN]]) for t in toe]
        t_hi = [sb(f"t_hi{s}", [P, 2, LEN], F32R) for s in range(2)]
        t_lo = [sb(f"t_lo{s}", [P, 2, LEN], F32R) for s in range(2)]
        y_hi = [sb(f"y_hi{s}", [P, CH, P], F32R) for s in range(2)]
        y_lo = [sb(f"y_lo{s}", [P, CH, P], F32R) for s in range(2)]
        result = [sb(f"result{s}", [P, LEN]) for s in range(2)]
        logits = sb("logits", [P, EXPERTS])
        top = sb("top", [P, 8])
        top_at = sb("top_at", [P, 8], U32)
        top_no = sb("top_no", [P, 2])
        held = sb("held", [P, 1])
        ratio = sb("ratio", [P, 1])
        half_sum = sb("half_sum", [P, 1])
        weight = sb("weight", [P, 2])
        gate1 = sb("gate1", [P, EXPERTS])
        gate2 = sb("gate2", [P, EXPERTS])
        gates = sb("gates", [P, EXPERTS])
        gated = sb("gated", [P, EXPERTS, RANK])
        gt_hi = sb("gt_hi", [P, P], F32R)
        gt_lo = sb("gt_lo", [P, P], F32R)
        mag = sb("mag", [P, KG, POS])
        turn = sb("turn", [P, KG, POS])
        wave = sb("wave", [P, KG, POS])
        wave2 = sb("wave2", [P, KG, NA])
        k_rows = sb("k_rows", [NA, KG, NB])
        prm = sb("prm", [P, 4, HEADS])
        pos = sb("pos", [P, POS])
        phase = sb("phase", [P, 4])
        d_row = sb("d_row", [NA, HEADS])
        d_one = sb("d_one", [NA, HEADS])
        logs = sb("logs", [HEADS, MODES + 1])
        exps = sb("exps", [HEADS, MODES + 1])
        ex_k = sb("ex_k", [HEADS, MODES + 1])
        ex_q = sb("ex_q", [HEADS, MODES + 1])
        ex_2k = sb("ex_2k", [HEADS, MODES + 1], I32)
        zeros = sb("zeros", [HEADS, P])
        len_i = sb("len_i", [P, SEQS], I32)
        len_f = sb("len_f", [P, SEQS])
        lang_i = sb("lang_i", [P, 1], I32)
        lang_f = sb("lang_f", [P, 1])
        sample_no = sb("sample_no", [P, CH])
        w_rows = result
        flat0, flat1 = [t[:, :, :].rearrange("p a b -> p (a b)") for t in toe]
        b_rows = flat1[:, 0:LEN].rearrange("p (e o r) -> p e o r", e=EXPERTS, o=8)
        b_sorted = flat1[:, LEN:2 * LEN].rearrange("p (o e r) -> p o e r", o=8, e=EXPERTS)
        (a_im, dt_re, dt_im, revs, back, sin1, sin_half, expo, tanh_half, em1, cos1, e_re, e_im, norm, t1, t2
         ) = [flat0[0:HEADS, n * MODES:(n + 1) * MODES] for n in range(16)]
        par = flat0[0:HEADS, LEN:LEN + 4 * P].rearrange("h (k q) -> h k q", k=4)
        c_in = flat0[0:HEADS, LEN + 4 * P:LEN + 5 * P].rearrange("h (n c) -> h n c", c=2)
        a_re, step_h = exps[:, 0:MODES], exps[:, MODES:MODES + 1]

        px = pb("px", [P, CH, P])
        pc = pb("pc", [P, 2, CH, SEQS])
        pm = pb("pm", [P, 3, 512])
        pg = pb("pg", [P, 512])
        k_psum = pg[0:NA, :].rearrange("a (h b) -> a h b", h=KG)
        w_psum = [px[:, :, :], pc[:, :, :, :].rearrange("p h c b -> p (h c b)").rearrange("p (c o) -> p c o", c=CH)]

        rows_in = [sem(f"rows_in{s}") for s in range(2)]
        toe_in = [sem(f"toe_in{s}") for s in range(2)]
        result_dma = [sem(f"result_dma{s}") for s in range(2)]
        px_full = sem("px_full")
        xt_ready = sem("xt_ready")
        uhi_ready = sem("uhi_ready")
        ulo_ready = sem("ulo_ready")
        thi_ready = sem("thi_ready")
        tlo_ready = sem("tlo_ready")
        conv_done = sem("conv_done")
        merged = sem("merged")
        yhi_ready = sem("yhi_ready")
        ylo_ready = sem("ylo_ready")
        gate_done = sem("gate_done")
        router = sem("router")
        ratio_ready = sem("ratio_ready")
        gated_ready = sem("gated_ready")
        gt_full = sem("gt_full")
        gthi_ready = sem("gthi_ready")
        gtlo_ready = sem("gtlo_ready")
        proj_done = sem("proj_done")
        pm_free = sem("pm_free")
        wt_full = sem("wt_full")
        whi_ready = sem("whi_ready")
        wlo_ready = sem("wlo_ready")
        b_in = sem("b_in")
        b_ready = sem("b_ready")
        par_in, small_in = sem("par_in"), sem("small_in")
        ident_ready = sem("ident_ready")
        consts = sem("consts")
        tables = sem("tables")
        par_act = sem("par_act")
        par_dve = sem("par_dve")
        prm_full, prm_ready = sem("prm_full"), sem("prm_ready")
        prod_ready = sem("prod_ready")
        angle_step = sem("angle_step")
        angle_ready = sem("angle_ready")
        mag_ready, wave_ready = sem("mag_ready"), sem("wave_ready")
        fac_step, fac_ready = sem("fac_step"), sem("fac_ready")
        k_full, k_copied, k_ready, k_stored = sem("k_full"), sem("k_copied"), sem("k_ready"), sem("k_stored")
        pad_stored = sem("pad_stored")

        block = ctx.enter_context(nc.Block())
        BODY = KG // 2
        LAST = PAIRS // BODY - 1
        WTILES = CH + 3
        W_LOADS = 16 * (CH // 2 + 1)
        ROUTER = 9
        TABLES = 7
        A_STEPS = 20
        PAR_STEPS = 59

        @block.sync
        def _(sp):
            sp.dma_start(logs[:, MODES:MODES + 1], log_dt.rearrange("(h a) -> h a", a=1)).then_inc(par_in, 16)
            sp.dma_start(logs[:, 0:MODES], log_A_real).then_inc(par_in, 16)
            sp.dma_start(a_im, A_imag).then_inc(par_in, 16)
            sp.dma_start(c_in, C).then_inc(par_in, 16)
            sp.wait_ge(tables, 1)
            sp.dma_start(d_row[NA - 1:NA, :], D.rearrange("(a h) -> a h", a=1)).then_inc(small_in, 16)
            for s in range(2):
                sp.dma_start(w_rows[s][:, :], W[s * P:(s + 1) * P, :]).then_inc(result_dma[s], 16)
            sp.dma_start(b_rows.rearrange("p e o r -> p e (o r)"),
                         B.rearrange("e (p o) r -> p e (o r)", o=8)).then_inc(b_in, 16)

            def load_rows(b, m):
                i, s = BODY * b + m, m % 2
                for h in range(2):
                    sp.dma_start(rows[s][h * SEQS:(h + 1) * SEQS, :],
                                 bass.AP(x.tensor, (2 * i + h) * LEN, [[HEADS * LEN, SEQS], [1, LEN]])
                                 ).then_inc(rows_in[s], 16)

            def load_toe(b, m):
                i, s = BODY * b + m, m % 2
                sp.dma_start(toe[s][:, :, :],
                             bass.AP(kpad.tensor, i * (2 * KPITCH), [[1, P], [KPITCH, 2], [1, LEN]])
                             ).then_inc(toe_in[s], 16)

            def store_kernels(g):
                sp.wait_ge(k_ready, g + 1)
                sp.dma_start(bass.AP(kpad.tensor, g * (KG * KPITCH), [[NB, NA], [KPITCH, KG], [1, NB]]),
                             k_rows[:, :, :]).then_inc(k_stored, 16)

            with sp.Fori(1, CH // 2) as j:
                for s in range(2):
                    sp.wait_ge(wt_full, 2 * j + (s - 1))
                    sp.dma_start(w_rows[s][:, :], W[bass.ds((2 * j + s) * P, P), :]).then_inc(result_dma[s], 16)
            sp.wait_ge(wt_full, CH - 1)
            sp.dma_start(w_rows[0][:, :], A.rearrange("e r d -> (e r) d")).then_inc(result_dma[0], 16)
            sp.wait_ge(wt_full, CH)
            sp.dma_start(w_rows[1][0:EXPERTS, :], Wr).then_inc(result_dma[1], 16)
            sp.dma_start(len_i[:, :], bass.AP(lengths.tensor, 0, [[0, P], [1, SEQS]])).then_inc(small_in, 16)
            for h in range(2):
                sp.dma_start(lang_i[h * SEQS:(h + 1) * SEQS, :],
                             languages.rearrange("(b a) -> b a", a=1)).then_inc(small_in, 16)
            for m in range(2):
                load_rows(0, m)
            sp.wait_ge(consts, 4)
            sp.dma_start(kpad[:, LEN:KPITCH], zeros[:, :]).then_inc(pad_stored, 16)
            store_kernels(0)
            sp.wait_ge(pad_stored, 16)
            sp.wait_ge(k_stored, 16)
            sp.wait_ge(prm_full, 1)
            load_toe(0, 0)
            sp.wait_ge(wt_full, WTILES)
            load_toe(0, 1)

            def step(b, m):
                i = BODY * b + m
                sp.wait_ge(px_full, i + 1)
                load_rows(b, m + 2)
                if m + 2 >= BODY:
                    sp.wait_ge(k_stored, 16 * b + 32)
                sp.wait_ge(thi_ready, i + 1)
                sp.wait_ge(tlo_ready, i + 1)
                load_toe(b, m + 2)

            with sp.Fori(0, LAST) as b:
                for m in range(BODY):
                    step(b, m)
                    if m == 1:
                        store_kernels(b + 1)
            for m in range(BODY - 2):
                sp.wait_ge(px_full, BODY * LAST + m + 1)
                load_rows(LAST, m + 2)
                sp.wait_ge(thi_ready, BODY * LAST + m + 1)
                sp.wait_ge(tlo_ready, BODY * LAST + m + 1)
                load_toe(LAST, m + 2)

        @block.gpsimd
        def _(pool):
            nc.gpsimd.memset(ident[:, :], 0.0).then_inc(consts, 1)
            pool.wait_ge(consts, 1)
            nc.gpsimd.affine_select(out=ident[:, :], in_=ident[:, :], compare_op=ALU.not_equal, fill=1.0,
                                    base=0, pattern=[[-1, P]], channel_multiplier=1).then_inc(ident_ready, 1)
            nc.gpsimd.iota(pos[:, 0:NB], [[-1, NB]], base=NB - 1, channel_multiplier=0,
                           allow_small_or_imprecise_dtypes=True).then_inc(consts, 1)
            nc.gpsimd.iota(pos[:, NB:POS], [[-NB, NA]], base=NB * (NA - 1), channel_multiplier=0,
                           allow_small_or_imprecise_dtypes=True).then_inc(consts, 1)
            nc.gpsimd.memset(zeros[:, :], 0.0).then_inc(consts, 1)
            nc.gpsimd.iota(sample_no[:, :], [[P, CH]], base=0, channel_multiplier=1,
                           allow_small_or_imprecise_dtypes=True).then_inc(consts, 1)
            nc.gpsimd.iota(expert_no[:, :], [[1, EXPERTS]], base=0, channel_multiplier=0,
                           allow_small_or_imprecise_dtypes=True).then_inc(consts, 1)
            for s in range(2):
                nc.gpsimd.memset(u_hi[s][:, 0:LEAD, :].bitcast(F32), 0.0).then_inc(consts, 1)
                nc.gpsimd.memset(u_lo[s][:, 0:LEAD, :].bitcast(F32), 0.0).then_inc(consts, 1)
            pool.wait_ge(b_in, 16)
            for e in range(EXPERTS):
                ins = nc.gpsimd.tensor_copy(b_sorted[:, :, e, :], b_rows[:, e, :, :])
            ins.then_inc(b_ready, 1)
            pool.wait_ge(consts, 6)
            pool.wait_ge(prm_ready, 1)

            def products(g):
                heads = bass.ds(g * KG, KG)
                at = pos[:, :].unsqueeze(1).to_broadcast([P, KG, POS])
                nc.gpsimd.tensor_tensor(turn[:, :, :], prm[:, 1, heads].unsqueeze(2).to_broadcast([P, KG, POS]),
                                        at, ALU.mult).then_inc(prod_ready, 1)
                nc.gpsimd.tensor_tensor(mag[:, :, :], prm[:, 0, heads].unsqueeze(2).to_broadcast([P, KG, POS]),
                                        at, ALU.mult).then_inc(prod_ready, 1)

            products(0)
            with pool.Fori(0, LAST) as b:
                pool.wait_ge(k_full, b + 1)
                products(b + 1)

        @block.scalar
        def _(act):
            act.wait_ge(par_dve, A_STEPS)
            nc.scalar.activation(tanh_half, dt_re, ACT.Tanh, scale=0.5).then_inc(par_act, 1)
            nc.scalar.activation(sin1, back, ACT.Sin, scale=-TWO_PI).then_inc(par_act, 1)
            nc.scalar.activation(sin_half, back, ACT.Sin, scale=-TWO_PI / 2).then_inc(par_act, 1)

            def weight(k, s, at, r, first=False):
                act.wait_ge(wt_full, k + 1)
                nc.scalar.activation(w_hi[:, :, at], w_psum[s][:, :, 0:r], ACT.Copy).then_inc(whi_ready, 1)

            def magnitudes(g):
                act.wait_ge(prod_ready, 2 * g + 2)
                nc.scalar.activation(mag[:, :, :], mag[:, :, :], ACT.Exp).then_inc(mag_ready, 1)

            def waves(g):
                act.wait_ge(angle_ready, g + 1)
                nc.scalar.activation(wave[:, :, :], wave[:, :, :], ACT.Sin, scale=-TWO_PI, bias=phase[:, 2:3]
                                     ).then_inc(wave_ready, 1)
                nc.scalar.activation(wave2[:, :, :], wave2[:, :, :], ACT.Sin, scale=-TWO_PI, bias=phase[:, 3:4]
                                     ).then_inc(wave_ready, 1)

            def copy_kernels(g):
                act.wait_ge(k_full, g + 1)
                nc.scalar.activation(k_rows[:, :, :], k_psum, ACT.Copy).then_inc(k_copied, 1)

            for k in range(2):
                weight(k, k, slice(k * P, (k + 1) * P), P)
            act.wait_ge(prm_full, 1)
            nc.scalar.activation(prm[:, :, :], pg[:, 0:4 * HEADS].rearrange("p (k h) -> p k h", k=4), ACT.Copy
                                 ).then_inc(prm_ready, 1)
            magnitudes(0)
            waves(0)
            with act.Fori(1, CH // 2) as j:
                for s in range(2):
                    weight(2 * j + s, s, bass.ds((2 * j + s) * P, P), P)
            copy_kernels(0)
            weight(CH, 0, slice(LEN, LEN + ER), P)
            weight(CH + 1, 1, slice(LEN + ER, WCOLS), EXPERTS)
            act.wait_ge(wt_full, WTILES)
            nc.scalar.activation(bt_hi[:, :].rearrange("e (p o) -> e o p", o=8), w_psum[0], ACT.Copy
                                 ).then_inc(whi_ready, 1)

            def split_rows(b, m, first=False):
                i, s = BODY * b + m, m % 2
                act.wait_ge(px_full, i + 1)
                if not first:
                    act.wait_ge(ylo_ready, i - 1)
                nc.scalar.activation(xt[s][:, :, :], px[:, :, :], ACT.Copy).then_inc(xt_ready, 1)
                if not first:
                    act.wait_ge(conv_done, i - 1)
                nc.scalar.activation(u_hi[s][:, LEAD:LEAD + CH, :], px[:, :, :], ACT.Copy).then_inc(uhi_ready, 1)

            def split_toe(b, m):
                s = m % 2
                act.wait_ge(toe_in[s], 32 * b + 16 * (m // 2 + 1))
                nc.scalar.activation(t_hi[s][:, :, :], toe_f[s], ACT.Copy).then_inc(thi_ready, 1)

            def split_y(b, m):
                s = m % 2
                act.wait_ge(merged, BODY * b + m + 1)
                nc.scalar.activation(y_hi[s][:, :, :], xt[s][:, :, :], ACT.Copy).then_inc(yhi_ready, 1)

            def finish(b, m):
                i, s = BODY * b + m, m % 2
                act.wait_ge(router, ROUTER * i + 2)
                nc.scalar.activation(ratio[:, :], top[:, 0:1], ACT.Exp, scale=-1.0, bias=top[:, 1:2]
                                     ).then_inc(ratio_ready, 1)
                act.wait_ge(gt_full, i + 1)
                nc.scalar.activation(gt_hi[:, :], pg[:, 0:P], ACT.Copy).then_inc(gthi_ready, 1)
                act.wait_ge(proj_done, i + 1)
                act.wait_ge(result_dma[s], W_LOADS + 64 * b + 32 * (m // 2))
                for n, (c0, c1) in enumerate(BANKS):
                    c1 = min(c1, LEN)
                    ins = nc.scalar.activation(result[s][:, c0:c1], pm[:, n, 0:c1 - c0], ACT.Copy)
                ins.then_inc(pm_free, 1)
                act.wait_ge(pm_free, i + 2)
                for h in range(2):
                    act.dma_start(bass.AP(out.tensor, (2 * i + h) * LEN, [[HEADS * LEN, SEQS], [1, LEN]]),
                                  result[s][h * SEQS:(h + 1) * SEQS, :]).then_inc(result_dma[s], 16)

            for m in range(2):
                split_rows(0, m, first=True)
            for m in range(2):
                split_toe(0, m)
            act.sem_inc(pm_free, 1)
            split_y(0, 0)

            def step(b, m, rows_left=True, kernels=True):
                if kernels and m == 0:
                    magnitudes(b + 1)
                    waves(b + 1)
                if rows_left:
                    split_rows(b, m + 2)
                if kernels and m == 1:
                    copy_kernels(b + 1)
                if rows_left:
                    act.wait_ge(conv_done, BODY * b + m + 1)
                    split_toe(b, m + 2)
                split_y(b, m + 1)
                finish(b, m)

            with act.Fori(0, LAST) as b:
                for m in range(BODY):
                    step(b, m)
            for m in range(BODY - 1):
                step(LAST, m, rows_left=m < BODY - 2, kernels=False)
            finish(LAST, BODY - 1)
            for s in range(2):
                act.wait_ge(result_dma[s], W_LOADS + 16 * PAIRS)

        @block.vector
        def _(dve):
            n_par = [0]

            def par_step(ins):
                n_par[0] += 1
                ins.then_inc(par_dve, 1)
                dve.wait_ge(par_dve, n_par[0])

            vec = nc.vector
            vec.memset(d_row[:, :], 0.0)
            vec.memset(phase[0:HEADS, 0:1], 0.25)
            vec.memset(phase[HEADS:P, 0:1], 0.0)
            vec.memset(phase[0:HEADS, 1:2], 0.0)
            vec.memset(phase[HEADS:P, 1:2], 0.25).then_inc(tables, 1)
            dve.wait_ge(tables, 1)
            vec.tensor_scalar(phase[:, 2:4], phase[:, 0:2], TWO_PI, None, ALU.mult).then_inc(tables, 1)

            def exact_exp(out, x, n):
                k, q, two_k = ex_k[:, 0:n], ex_q[:, 0:n], ex_2k[:, 0:n]
                par_step(vec.tensor_scalar(k, x, 1.0 / math.log(2.0), MAGIC, ALU.mult, ALU.add))
                par_step(vec.tensor_scalar(k, k, MAGIC, -126.0, ALU.subtract, ALU.max))
                par_step(vec.tensor_scalar(k, k, 127.0, None, ALU.min))
                par_step(vec.tensor_scalar(two_k, k, 127.0, 2.0 ** 23, ALU.add, ALU.mult))
                par_step(vec.scalar_tensor_tensor(out=out, in0=k, scalar=-LN2_HI, in1=x, op0=ALU.mult, op1=ALU.add))
                par_step(vec.scalar_tensor_tensor(out=out, in0=k, scalar=-LN2_LO, in1=out, op0=ALU.mult, op1=ALU.add))
                par_step(vec.tensor_scalar(q, out, 1.0 / math.factorial(7), None, ALU.mult))
                for m in range(6, 0, -1):
                    par_step(vec.scalar_tensor_tensor(out=q, in0=q, scalar=1.0 / math.factorial(m), in1=out,
                                                      op0=ALU.add, op1=ALU.mult))
                par_step(vec.scalar_tensor_tensor(out=out, in0=q, scalar=1.0, in1=two_k.bitcast(F32),
                                                  op0=ALU.add, op1=ALU.mult))

            dve.wait_ge(par_in, 64)
            exact_exp(exps[:, :], logs[:, :], MODES + 1)
            par_step(vec.tensor_scalar(dt_im, a_im, step_h[:, :], None, ALU.mult))
            par_step(vec.tensor_scalar(dt_re, a_re, step_h[:, :], -1.0, ALU.mult, ALU.mult))
            par_step(vec.tensor_scalar(revs, dt_im, 1.0 / (2.0 * math.pi), None, ALU.mult))
            par_step(vec.tensor_scalar(t1, revs, MAGIC, None, ALU.add))
            par_step(vec.tensor_scalar(t2, t1, MAGIC, None, ALU.subtract))
            par_step(vec.tensor_tensor(back, t2, revs, ALU.subtract))
            assert n_par[0] == A_STEPS
            exact_exp(expo, dt_re, MODES)
            par_step(vec.tensor_tensor(t1, a_re, a_re, ALU.mult))
            par_step(vec.tensor_tensor(t2, a_im, a_im, ALU.mult))
            par_step(vec.tensor_tensor(norm, t1, t2, ALU.add))
            par_step(vec.reciprocal(norm, norm))
            dve.wait_ge(par_act, 1)
            par_step(vec.scalar_tensor_tensor(out=em1, in0=expo, scalar=1.0, in1=tanh_half, op0=ALU.add, op1=ALU.mult))
            dve.wait_ge(par_act, 3)
            par_step(vec.scalar_tensor_tensor(out=cos1, in0=sin_half, scalar=-2.0, in1=sin_half, op0=ALU.mult, op1=ALU.mult))
            par_step(vec.scalar_tensor_tensor(out=t1, in0=cos1, scalar=1.0, in1=em1, op0=ALU.add, op1=ALU.mult))
            par_step(vec.tensor_tensor(e_re, t1, cos1, ALU.add))
            par_step(vec.tensor_tensor(e_im, expo, sin1, ALU.mult))
            q_re, q_im = revs, em1
            par_step(vec.scalar_tensor_tensor(out=t1, in0=e_re, scalar=-1.0, in1=a_re, op0=ALU.mult, op1=ALU.mult))
            par_step(vec.tensor_tensor(t2, e_im, a_im, ALU.mult))
            par_step(vec.tensor_tensor(t1, t1, t2, ALU.add))
            par_step(vec.tensor_tensor(q_re, t1, norm, ALU.mult))
            par_step(vec.scalar_tensor_tensor(out=t1, in0=e_im, scalar=-1.0, in1=a_re, op0=ALU.mult, op1=ALU.mult))
            par_step(vec.tensor_tensor(t2, e_re, a_im, ALU.mult))
            par_step(vec.tensor_tensor(t1, t1, t2, ALU.subtract))
            par_step(vec.tensor_tensor(q_im, t1, norm, ALU.mult))
            par_step(vec.tensor_tensor(t1, c_in[:, :, 0], q_re, ALU.mult))
            par_step(vec.tensor_tensor(t2, c_in[:, :, 1], q_im, ALU.mult))
            par_step(vec.tensor_tensor(t1, t1, t2, ALU.subtract))
            vec.tensor_scalar(par[:, 2, 0:MODES], t1, 2.0, None, ALU.mult)
            par_step(vec.tensor_scalar(par[:, 2, MODES:P], t1, -2.0, None, ALU.mult))
            par_step(vec.tensor_tensor(t1, c_in[:, :, 0], q_im, ALU.mult))
            par_step(vec.tensor_tensor(t2, c_in[:, :, 1], q_re, ALU.mult))
            par_step(vec.tensor_tensor(t1, t1, t2, ALU.add))
            for half in (slice(0, MODES), slice(MODES, P)):
                vec.tensor_scalar(par[:, 3, half], t1, -2.0, None, ALU.mult)
                vec.tensor_scalar(par[:, 1, half], back, -1.0, None, ALU.mult)
                ins = vec.tensor_scalar(par[:, 0, half], dt_re, 1.0, None, ALU.mult)
            par_step(ins)
            assert n_par[0] == PAR_STEPS
            def low_weight(k, s, at, r):
                dve.wait_ge(whi_ready, k + 1)
                vec.tensor_tensor(w_lo[:, :, at], w_psum[s][:, :, 0:r], w_hi[:, :, at].bitcast(F32), ALU.subtract
                                  ).then_inc(wlo_ready, 1)

            def angles(g):
                far = turn[:, :, NB:POS]
                dve.wait_ge(prod_ready, 2 * g + 1)
                vec.tensor_scalar(wave[:, :, :], turn[:, :, :], phase[:, 0:1], MAGIC, ALU.add, ALU.add
                                  ).then_inc(angle_step, 1)
                vec.tensor_scalar(wave2[:, :, :], far, phase[:, 1:2], MAGIC, ALU.add, ALU.add).then_inc(angle_step, 1)
                dve.wait_ge(angle_step, 2 * g + 2)
                vec.scalar_tensor_tensor(out=wave[:, :, :], in0=wave[:, :, :], scalar=MAGIC, in1=turn[:, :, :],
                                         op0=ALU.subtract, op1=ALU.subtract)
                vec.scalar_tensor_tensor(out=wave2[:, :, :], in0=wave2[:, :, :], scalar=MAGIC, in1=far,
                                         op0=ALU.subtract, op1=ALU.subtract).then_inc(angle_ready, 1)

            def factors(g):
                heads = bass.ds(g * KG, KG)
                far = wave[:, :, NB:POS]
                dve.wait_ge(wave_ready, 2 * g + 2)
                dve.wait_ge(mag_ready, g + 1)
                vec.tensor_tensor(far, far, prm[:, 2, heads].unsqueeze(2).to_broadcast([P, KG, NA]), ALU.mult
                                  ).then_inc(fac_step, 1)
                vec.tensor_tensor(wave2[:, :, :], wave2[:, :, :],
                                  prm[:, 3, heads].unsqueeze(2).to_broadcast([P, KG, NA]), ALU.mult
                                  ).then_inc(fac_step, 1)
                dve.wait_ge(fac_step, 3 * g + 2)
                vec.tensor_tensor(far, far, wave2[:, :, :], ALU.add).then_inc(fac_step, 1)
                dve.wait_ge(fac_step, 3 * g + 3)
                vec.tensor_tensor(wave[:, :, :], wave[:, :, :], mag[:, :, :], ALU.mult).then_inc(fac_ready, 1)

            def first_samples(g):
                dve.wait_ge(k_copied, g + 1)
                at0 = k_rows[:, :, NB - 1:NB].rearrange("p h q -> p (h q)")
                vec.tensor_tensor(at0, at0, d_one[:, bass.ds(g * KG, KG)], ALU.add).then_inc(k_ready, 1)

            for k in range(2):
                low_weight(k, k, slice(k * P, (k + 1) * P), P)
            angles(0)
            with dve.Fori(1, CH // 2) as j:
                for s in range(2):
                    low_weight(2 * j + s, s, bass.ds((2 * j + s) * P, P), P)
            factors(0)
            low_weight(CH, 0, slice(LEN, LEN + ER), P)
            low_weight(CH + 1, 1, slice(LEN + ER, WCOLS), EXPERTS)
            dve.wait_ge(small_in, 64)
            dve.wait_ge(consts, 6)
            dve.wait_ge(ident_ready, 1)
            vec.tensor_scalar(d_one[:, :], d_row[:, :], ident[0:NA, NA - 1:NA], None, ALU.add).then_inc(tables, 1)
            vec.tensor_copy(len_f[:, :], len_i[:, :]).then_inc(tables, 1)
            vec.tensor_copy(lang_f[:, :], lang_i[:, :]).then_inc(tables, 1)
            dve.wait_ge(tables, 5)
            first_samples(0)
            dve.wait_ge(whi_ready, WTILES)
            bt_view = [t[:, :].rearrange("e (p o) -> e o p", o=8) for t in (bt_lo, bt_hi)]
            vec.tensor_tensor(bt_view[0], w_psum[0], bt_view[1].bitcast(F32), ALU.subtract).then_inc(wlo_ready, 1)
            vec.tensor_tensor(valid[:, :, :], sample_no[:, :].unsqueeze(2).to_broadcast([P, CH, SEQS]),
                              len_f[:, :].unsqueeze(1).to_broadcast([P, CH, SEQS]), ALU.is_lt).then_inc(tables, 1)
            vec.tensor_scalar(bias[:, :], expert_no[:, :], lang_f[:, :], LANG_BIAS, ALU.is_equal, ALU.mult
                              ).then_inc(tables, 1)

            def split_rows(b, m, first=False):
                i, s = BODY * b + m, m % 2
                dve.wait_ge(xt_ready, i + 1)
                dve.wait_ge(uhi_ready, i + 1)
                if not first:
                    dve.wait_ge(conv_done, i - 1)
                at = slice(LEAD, LEAD + CH)
                vec.tensor_tensor(u_lo[s][:, at, :], xt[s][:, :, :], u_hi[s][:, at, :].bitcast(F32), ALU.subtract
                                  ).then_inc(ulo_ready, 1)

            def split_toe(b, m):
                s = m % 2
                dve.wait_ge(thi_ready, BODY * b + m + 1)
                vec.tensor_tensor(t_lo[s][:, :, :], toe_f[s], t_hi[s][:, :, :].bitcast(F32), ALU.subtract
                                  ).then_inc(tlo_ready, 1)

            def hold():
                vec.tensor_copy(held[:, :], lang_f[:, :])

            def merge(b, m):
                i, s = BODY * b + m, m % 2
                dve.wait_ge(ulo_ready, i + 1)
                dve.wait_ge(conv_done, i + 1)
                hold()
                for h in range(2):
                    ins = vec.copy_predicated(xt[s][:, :, h * SEQS:(h + 1) * SEQS], valid[:, :, :], pc[:, h, :, :])
                ins.then_inc(merged, 1)
                dve.wait_ge(yhi_ready, i + 1)
                vec.tensor_tensor(y_lo[s][:, :, :], xt[s][:, :, :], y_hi[s][:, :, :].bitcast(F32), ALU.subtract
                                  ).then_inc(ylo_ready, 1)

            def route(b, m):
                i = BODY * b + m
                gate = pm[:, 2, :]
                base = ROUTER * i
                dve.wait_ge(gate_done, i + 1)
                vec.tensor_tensor(logits[:, :], gate[:, L0:L0 + EXPERTS], bias[:, :], ALU.add).then_inc(router, 1)
                dve.wait_ge(router, base + 1)
                hold()
                vec.max(top[:, :], logits[:, :]).then_inc(router, 1)
                dve.wait_ge(router, base + 2)
                hold()
                vec.max_index(top_at[:, :], top[:, :], logits[:, :]).then_inc(router, 1)
                dve.wait_ge(router, base + 3)
                vec.tensor_copy(top_no[:, :], top_at[:, 0:2]).then_inc(router, 1)
                dve.wait_ge(ratio_ready, i + 1)
                vec.tensor_scalar(half_sum[:, :], ratio[:, :], 1.0 / SCALING, 1.0 / SCALING, ALU.mult, ALU.add
                                  ).then_inc(router, 1)
                dve.wait_ge(router, base + 5)
                vec.reciprocal(weight[:, 0:1], half_sum[:, :]).then_inc(router, 1)
                dve.wait_ge(router, base + 6)
                vec.tensor_tensor(weight[:, 1:2], weight[:, 0:1], ratio[:, :], ALU.mult).then_inc(router, 1)
                vec.tensor_scalar(gate1[:, :], expert_no[:, :], top_no[:, 0:1], weight[:, 0:1],
                                  ALU.is_equal, ALU.mult)
                dve.wait_ge(router, base + 7)
                vec.tensor_scalar(gate2[:, :], expert_no[:, :], top_no[:, 1:2], weight[:, 1:2],
                                  ALU.is_equal, ALU.mult).then_inc(router, 1)
                dve.wait_ge(router, base + 8)
                vec.tensor_tensor(gates[:, :], gate1[:, :], gate2[:, :], ALU.add).then_inc(router, 1)
                dve.wait_ge(router, base + 9)
                vec.tensor_tensor(gated[:, :, :], gate[:, H0:L0].rearrange("p (e r) -> p e r", e=EXPERTS),
                                  gates[:, :].unsqueeze(2).to_broadcast([P, EXPERTS, RANK]), ALU.mult
                                  ).then_inc(gated_ready, 1)
                dve.wait_ge(gthi_ready, i + 1)
                vec.tensor_tensor(gt_lo[:, :], pg[:, 0:P], gt_hi[:, :].bitcast(F32), ALU.subtract
                                  ).then_inc(gtlo_ready, 1)

            dve.wait_ge(tables, TABLES)
            for m in range(2):
                split_rows(0, m, first=True)
            for m in range(2):
                split_toe(0, m)
            merge(0, 0)

            def step(b, m, rows_left=True, kernels=True):
                if kernels and m == 0:
                    angles(b + 1)
                if rows_left:
                    split_rows(b, m + 2)
                    if kernels and m == 1:
                        first_samples(b + 1)
                    split_toe(b, m + 2)
                if kernels and m == 0:
                    factors(b + 1)
                merge(b, m + 1)
                route(b, m)

            with dve.Fori(0, LAST) as b:
                for m in range(BODY):
                    step(b, m)
            for m in range(BODY - 1):
                step(LAST, m, rows_left=m < BODY - 2, kernels=False)
            route(LAST, BODY - 1)

        @block.tensor
        def _(pe):
            pe.wait_ge(ident_ready, 1)

            def turn_weight(k, s, r, k_in, diagonal=False, first=False):
                pe.wait_ge(result_dma[s], k_in)
                if not first:
                    pe.wait_ge(wlo_ready, k - 1)
                for c in range(CH):
                    ins = nc.tensor.matmul(w_psum[s][:, c, 0:r], w_rows[s][0:r, c * P:(c + 1) * P],
                                           ident[0:r, 0:r], is_transpose=True, start=c % 4 == 0, stop=True,
                                           skip_group_check=True)
                if diagonal:
                    tile = w_psum[s][:, bass.ds(k, 1), :].rearrange("p a o -> p (a o)")
                    ins = nc.tensor.matmul(tile, ident[:, :], ident[:, :], start=False, stop=True,
                                           skip_group_check=True)
                ins.then_inc(wt_full, 1)

            def make_kernels(g):
                pe.wait_ge(fac_ready, g + 1)
                for h in range(KG):
                    ins = nc.tensor.matmul(k_psum[:, h, :], wave[:, h, NB:POS], wave[:, h, 0:NB],
                                           start=True, stop=True)
                ins.then_inc(k_full, 1)

            for k in range(2):
                turn_weight(k, k, P, 16, diagonal=True, first=True)
            pe.wait_ge(par_dve, PAR_STEPS)
            for k in range(4):
                ins = nc.tensor.transpose(pg[:, k * HEADS:(k + 1) * HEADS], par[:, k, :], ident[0:HEADS, 0:HEADS])
            ins.then_inc(prm_full, 1)
            with pe.Fori(1, CH // 2) as j:
                for s in range(2):
                    turn_weight(2 * j + s, s, P, 16 * j + 16, diagonal=True)
            pe.wait_ge(prm_ready, 1)
            make_kernels(0)
            turn_weight(CH, 0, P, W_LOADS)
            turn_weight(CH + 1, 1, EXPERTS, W_LOADS)
            pe.wait_ge(b_ready, 1)
            pe.wait_ge(wlo_ready, CH + 1)
            for o in range(8):
                ins = nc.tensor.transpose(w_psum[0][:, o, :], b_sorted[:, o, :, :].rearrange("p e r -> p (e r)"),
                                          ident[:, :])
            ins.then_inc(wt_full, 1)

            def turn_rows(b, m, first=False):
                i, s = BODY * b + m, m % 2
                pe.wait_ge(rows_in[s], 64 * b + 32 * (m // 2 + 1))
                if first:
                    pe.wait_ge(wlo_ready, WTILES)
                else:
                    pe.wait_ge(uhi_ready, i)
                for c in range(CH):
                    ins = nc.tensor.transpose(px[:, c, :], rows[s][:, c * P:(c + 1) * P], ident[:, :])
                ins.then_inc(px_full, 1)

            def convolve(b, m, first=False):
                i, s = BODY * b + m, m % 2
                pe.wait_ge(uhi_ready, i + 1)
                pe.wait_ge(ulo_ready, i + 1)
                pe.wait_ge(thi_ready, i + 1)
                pe.wait_ge(tlo_ready, i + 1)
                if first:
                    pe.wait_ge(consts, 10)
                else:
                    pe.wait_ge(merged, i)
                for h in range(2):
                    tok = slice(h * SEQS, (h + 1) * SEQS)
                    for d in range(CH):
                        lead = max(0, d - (CH - 1 - LEAD))
                        n = CH - d + lead
                        for t, u in ((t_hi, u_hi), (t_hi, u_lo), (t_lo, u_hi)):
                            ins = nc.tensor.matmul(pc[:, h, CH - n:CH, :], t[s][:, h, d * P:(d + 1) * P],
                                                   u[s][:, LEAD - lead:LEAD - lead + n, tok],
                                                   start=(d == 0 and u is u_hi and t is t_hi),
                                                   stop=(d == CH - 1 and t is t_lo))
                ins.then_inc(conv_done, 1)

            def project(b, m):
                i, s = BODY * b + m, m % 2
                pe.wait_ge(yhi_ready, i + 1)
                pe.wait_ge(ylo_ready, i + 1)
                pe.wait_ge(pm_free, i + 1)
                for n in (2, 0, 1):
                    c0, c1 = BANKS[n]
                    for c in range(CH):
                        if n == 1 and c == CH // 2:
                            pe.wait_ge(gated_ready, i + 1)
                            if m == 1:
                                pe.wait_ge(k_copied, b + 2 if b is not LAST else KGROUPS)
                            nc.tensor.transpose(pg[:, 0:P], gated[:, :, :].rearrange("p e r -> p (e r)"), ident[:, :]
                                                ).then_inc(gt_full, 1)
                        for y, w in ((y_hi, w_hi), (y_lo, w_hi), (y_hi, w_lo)):
                            ins = nc.tensor.matmul(pm[:, n, 0:c1 - c0], y[s][:, c, :], w[:, c, c0:c1],
                                                   start=(c == 0 and y is y_hi and w is w_hi),
                                                   stop=(c == CH - 1 and w is w_lo), skip_group_check=True)
                    if n == 2:
                        ins.then_inc(gate_done, 1)
                pe.wait_ge(gthi_ready, i + 1)
                pe.wait_ge(gtlo_ready, i + 1)
                for n, (c0, c1) in enumerate(BANKS):
                    c1 = min(c1, LEN)
                    for g, w in ((gt_hi, bt_hi), (gt_lo, bt_hi), (gt_hi, bt_lo)):
                        ins = nc.tensor.matmul(pm[:, n, 0:c1 - c0], g[:, :], w[:, c0:c1], start=False,
                                               stop=w is bt_lo, skip_group_check=True)
                ins.then_inc(proj_done, 1)

            for m in range(2):
                turn_rows(0, m, first=m == 0)
            convolve(0, 0, first=True)

            def step(b, m, rows_left=True, kernels=True):
                if kernels and m == 1:
                    make_kernels(b + 1)
                if rows_left:
                    turn_rows(b, m + 2)
                convolve(b, m + 1)
                project(b, m)

            with pe.Fori(0, LAST) as b:
                for m in range(BODY):
                    step(b, m)
            for m in range(BODY - 1):
                step(LAST, m, rows_left=m < BODY - 2, kernels=False)
            project(LAST, BODY - 1)


_INS = ["x", "itok_B_8_3872", "itok_B_0_7", "L0_cond_log_dt", "L0_cond_C", "L0_cond_log_A_real", "L0_cond_A_imag",
        "L0_cond_D", "L1_cond_W", "L1_cond_Wr", "L1_cond_A", "L1_cond_B"]


def kernel(**inputs):
    import numpy as _np
    import concourse.bacc as _bacc
    from concourse import mybir as _mybir
    from concourse.bass_utils import run_bass_kernel_spmd as _run

    nc = _bacc.Bacc("TRN2", target_bir_lowering=False, num_devices=1)
    arrays, args = {}, []
    for name in _INS:
        a = _np.ascontiguousarray(inputs[name])
        arrays[f"in_{name}"] = a
        args.append(nc.dram_tensor(f"in_{name}", a.shape, _mybir.dt.from_np(a.dtype), kind="ExternalInput").ap())
    args.append(nc.dram_tensor("out_0", (SEQS, HEADS, LEN), _mybir.dt.float32, kind="ExternalOutput").ap())
    cond_resid_kernel(nc, *args)
    r = _run(nc, [arrays], core_ids=[0])
    return r.results[0]["out_0"]
```

```python
import math
from contextlib import ExitStack

import concourse.bass as bass
from concourse import mybir

F32 = mybir.dt.float32
F32R = mybir.dt.float32r
I32 = mybir.dt.int32
U32 = mybir.dt.uint32
ALU = mybir.AluOpType
ACT = mybir.ActivationFunctionType

P = 128
SEQS, HEADS, LEN = 64, 64, 1024
MODES = 64
CH = LEN // P
PAIRS = HEADS // 2
LEAD = 2
EXPERTS, RANK = 8, 16
ER = EXPERTS * RANK
LANG_BIAS, SCALING = 5.0, 2.0
WCOLS = LEN + ER + EXPERTS
BANKS = [(0, 388), (388, 776), (776, WCOLS)]
GATE = BANKS[2]
H0 = LEN - GATE[0]
L0 = H0 + ER
KPITCH = LEN + P

NA, NB = 16, 64
POS = NB + NA
KG = 8
KGROUPS = HEADS // KG
MAGIC = 1.5 * 2.0 ** 23
LN2_HI, LN2_LO = 0.693359375, -2.12194440054690583e-4
TWO_PI = 6.283185


def cond_resid_kernel(nc, x, lengths, languages, log_dt, C, log_A_real, A_imag, D, W, Wr, A, B, out):
    kpad = nc.dram_tensor("kpad", (HEADS, KPITCH), F32, kind="Internal").ap()
    with ExitStack() as ctx:
        def sb(name, shape, dt=F32):
            return ctx.enter_context(nc.sbuf_tensor(name, shape, dt))

        def pb(name, shape):
            return ctx.enter_context(nc.psum_tensor(name, shape, F32))

        def sem(name):
            return ctx.enter_context(nc.semaphore(name))

        w_hi = sb("w_hi", [P, CH, WCOLS], F32R)
        w_lo = sb("w_lo", [P, CH, WCOLS], F32R)
        bt_hi = sb("bt_hi", [P, LEN], F32R)
        bt_lo = sb("bt_lo", [P, LEN], F32R)
        valid = sb("valid", [P, CH, SEQS], I32)
        bias = sb("bias", [P, EXPERTS])
        ident = sb("ident", [P, P])
        expert_no = sb("expert_no", [P, EXPERTS])
        rows = [sb(f"rows{s}", [P, LEN]) for s in range(2)]
        xt = [sb(f"xt{s}", [P, CH, P]) for s in range(2)]
        u_hi = [sb(f"u_hi{s}", [P, LEAD + CH, P], F32R) for s in range(2)]
        u_lo = [sb(f"u_lo{s}", [P, LEAD + CH, P], F32R) for s in range(2)]
        toe = [sb(f"toe{s}", [P, 2, LEN]) for s in range(2)]
        toe_f = [bass.AP(t[:, :, :].tensor, LEN - 1, [[2 * LEN, P], [LEN, 2], [-1, LEN]]) for t in toe]
        t_hi = [sb(f"t_hi{s}", [P, 2, LEN], F32R) for s in range(2)]
        t_lo = [sb(f"t_lo{s}", [P, 2, LEN], F32R) for s in range(2)]
        y_hi = [sb(f"y_hi{s}", [P, CH, P], F32R) for s in range(2)]
        y_lo = [sb(f"y_lo{s}", [P, CH, P], F32R) for s in range(2)]
        result = [sb(f"result{s}", [P, LEN]) for s in range(2)]
        logits = sb("logits", [P, EXPERTS])
        top = sb("top", [P, 8])
        top_at = sb("top_at", [P, 8], U32)
        top_no = sb("top_no", [P, 2])
        held = sb("held", [P, 1])
        ratio = sb("ratio", [P, 1])
        half_sum = sb("half_sum", [P, 1])
        weight = sb("weight", [P, 2])
        gate1 = sb("gate1", [P, EXPERTS])
        gate2 = sb("gate2", [P, EXPERTS])
        gates = sb("gates", [P, EXPERTS])
        gated = sb("gated", [P, EXPERTS, RANK])
        gt_hi = sb("gt_hi", [P, P], F32R)
        gt_lo = sb("gt_lo", [P, P], F32R)
        mag = sb("mag", [P, KG, POS])
        turn = sb("turn", [P, KG, POS])
        wave = sb("wave", [P, KG, POS])
        wave2 = sb("wave2", [P, KG, NA])
        k_rows = sb("k_rows", [NA, KG, NB])
        prm = sb("prm", [P, 4, HEADS])
        pos = sb("pos", [P, POS])
        phase = sb("phase", [P, 4])
        d_row = sb("d_row", [NA, HEADS])
        d_one = sb("d_one", [NA, HEADS])
        logs = sb("logs", [HEADS, MODES + 1])
        exps = sb("exps", [HEADS, MODES + 1])
        ex_k = sb("ex_k", [HEADS, MODES + 1])
        ex_q = sb("ex_q", [HEADS, MODES + 1])
        ex_2k = sb("ex_2k", [HEADS, MODES + 1], I32)
        zeros = sb("zeros", [HEADS, P])
        len_i = sb("len_i", [P, SEQS], I32)
        len_f = sb("len_f", [P, SEQS])
        lang_i = sb("lang_i", [P, 1], I32)
        lang_f = sb("lang_f", [P, 1])
        sample_no = sb("sample_no", [P, CH])
        wr_rows = sb("wr_rows", [CH * EXPERTS, P])
        half1 = [toe[1][:, h, :] for h in range(2)]
        b_rows = half1[0].rearrange("p (e o r) -> p e o r", e=EXPERTS, o=8)
        b_sorted = half1[1].rearrange("p (o e r) -> p o e r", o=8, e=EXPERTS)
        xt1_rows = xt[1][:, :, :].rearrange("p c t -> p (c t)")
        w_rows = [rows[1][:, :], result[0][:, :], result[1][:, :], xt1_rows] + half1 + [result[0][:, :], result[1][:, :]]
        a_rows = rows[0][:, :]
        flat0 = toe[0][:, :, :].rearrange("p a b -> p (a b)")
        (a_im, dt_im, revs, whole, sin1, sin_half, expo, tanh_half, em1, cos1, e_re, e_im, norm, n_re, n_im, g_re,
         g_im, t1, t2, t3, t4) = [flat0[0:HEADS, n * MODES:(n + 1) * MODES] for n in range(21)]
        par = flat0[0:HEADS, 21 * MODES:29 * MODES].rearrange("h (k q) -> h k q", k=4)
        c_in = flat0[0:HEADS, 29 * MODES:31 * MODES].rearrange("h (n c) -> h n c", c=2)
        halves = (slice(0, MODES), slice(MODES, P))
        dt_re, turns = par[:, 0, 0:MODES], par[:, 1, 0:MODES]
        a_re, step_h = exps[:, 0:MODES], exps[:, MODES:MODES + 1]

        px = pb("px", [P, CH, P])
        pc = pb("pc", [P, 2, CH, SEQS])
        pmg = pb("pmg", [P, 4, 512])
        pm = pmg[:, 0:3, :]
        pg = pmg[:, 3, :]
        k_psum = pg[0:NA, :].rearrange("a (h b) -> a h b", h=KG)
        in_pc = pc[:, :, :, :].rearrange("p h c b -> p (h c b)").rearrange("p (c o) -> p c o", c=CH)
        in_pm = pm[:, 0:2, :].rearrange("p n f -> p (n f)").rearrange("p (c o) -> p c o", c=CH)
        in_pg = pmg[:, 2:4, :].rearrange("p n f -> p (n f)").rearrange("p (c o) -> p c o", c=CH)
        in_px = px[:, :, :]
        W_, A_, WR_, B_ = range(4)
        places = [(W_, in_pc), (W_, in_pm), (W_, in_px), (WR_, in_pg), (B_, in_pc), (W_, in_pm), (W_, in_px),
                  (A_, in_pg), (W_, in_pc), (W_, in_pm), (W_, in_px)]
        TILE = []
        for what, place in places:
            c0 = {W_: P * sum(t[0] == W_ for t in TILE), A_: LEN, WR_: LEN + ER, B_: 0}[what]
            TILE.append((what, place, slice(c0, c0 + (EXPERTS if what == WR_ else P))))
        X1_TURN = 9

        def w_tile(n):
            return [k for k, t in enumerate(TILE) if t[0] == W_][n]

        def tile_views(k, wide, narrow):
            what, place, at = TILE[k]
            if what == B_:
                return place, narrow[:, :].rearrange("e (p o) -> e o p", o=8)
            if what == WR_:
                place = place.rearrange("p c o -> p (c o)")[:, 0:CH * EXPERTS].rearrange("p (c e) -> p c e", c=CH)
            return place, wide[:, :, at]

        rows_in = [sem(f"rows_in{s}") for s in range(2)]
        toe_half = sem("toe_half")
        toe_in = [sem(f"toe_in{s}") for s in range(2)]
        result_dma = [sem(f"result_dma{s}") for s in range(2)]
        px_full = sem("px_full")
        xt_ready = sem("xt_ready")
        uhi_ready = sem("uhi_ready")
        ulo_ready = sem("ulo_ready")
        thi_ready = sem("thi_ready")
        tlo_ready = sem("tlo_ready")
        conv_done = sem("conv_done")
        merged = sem("merged")
        yhi_ready = sem("yhi_ready")
        ylo_ready = sem("ylo_ready")
        gate_done = sem("gate_done")
        router = sem("router")
        ratio_ready = sem("ratio_ready")
        gated_ready = sem("gated_ready")
        gt_full = sem("gt_full")
        gthi_ready = sem("gthi_ready")
        gtlo_ready = sem("gtlo_ready")
        proj_done = sem("proj_done")
        pm_free = sem("pm_free")
        wt_full = sem("wt_full")
        whi_ready = sem("whi_ready")
        wlo_ready = sem("wlo_ready")
        w_in = [sem(f"w_in{n}") for n in range(CH)]
        a_in, b_in, wr_in = sem("a_in"), sem("b_in"), sem("wr_in")
        b_ready = sem("b_ready")
        thi_half, tlo_half = sem("thi_half"), sem("tlo_half")
        logs_in, par_in, d_in, small_in = sem("logs_in"), sem("par_in"), sem("d_in"), sem("small_in")
        ident_ready = sem("ident_ready")
        consts = sem("consts")
        tables = sem("tables")
        par_act = sem("par_act")
        par_dve = sem("par_dve")
        prm_full, prm_ready = sem("prm_full"), sem("prm_ready")
        prod_ready = sem("prod_ready")
        angle_step = sem("angle_step")
        angle_ready = sem("angle_ready")
        mag_ready, wave_ready = sem("mag_ready"), sem("wave_ready")
        fac_step, fac_ready = sem("fac_step"), sem("fac_ready")
        k_full, k_copied, k_ready, k_stored = sem("k_full"), sem("k_copied"), sem("k_ready"), sem("k_stored")
        pad_stored = sem("pad_stored")

        block = ctx.enter_context(nc.Block())
        BODY = KG // 2
        LAST = PAIRS // BODY - 1
        WTILES = len(TILE)
        TILE_A, TILE_B = [[t[0] for t in TILE].index(what) for what in (A_, B_)]
        START = 16
        ROUTER = 9
        TABLES = 7
        A_STEPS = 25
        PAR_STEPS = 61

        @block.sync
        def _(sp):
            sp.dma_start(logs[:, MODES:MODES + 1], log_dt.rearrange("(h a) -> h a", a=1)).then_inc(logs_in, 16)
            sp.dma_start(logs[:, 0:MODES], log_A_real).then_inc(logs_in, 16)
            sp.dma_start(a_im, A_imag).then_inc(par_in, 16)
            sp.dma_start(c_in, C).then_inc(par_in, 16)
            def load_rows(b, m):
                i, s = BODY * b + m, m % 2
                for h in range(2):
                    sp.dma_start(rows[s][h * SEQS:(h + 1) * SEQS, :],
                                 bass.AP(x.tensor, (2 * i + h) * LEN, [[HEADS * LEN, SEQS], [1, LEN]])
                                 ).then_inc(rows_in[s], 16)

            def load_toe(b, m):
                i, s = BODY * b + m, m % 2
                sp.dma_start(toe[s][:, :, :],
                             bass.AP(kpad.tensor, i * (2 * KPITCH), [[1, P], [KPITCH, 2], [1, LEN]])
                             ).then_inc(toe_in[s], 16)

            def store_kernels(g):
                sp.wait_ge(k_ready, g + 1)
                sp.dma_start(bass.AP(kpad.tensor, g * (KG * KPITCH), [[NB, NA], [KPITCH, KG], [1, NB]]),
                             k_rows[:, :, :]).then_inc(k_stored, 16)

            def load_w(n):
                sp.dma_start(w_rows[n], W[n * P:(n + 1) * P, :]).then_inc(w_in[n], 16)

            load_rows(0, 0)
            sp.dma_start(b_rows.rearrange("p e o r -> p e (o r)"),
                         B.rearrange("e (p o) r -> p e (o r)", o=8)).then_inc(b_in, 16)
            for n in range(4):
                load_w(n)
            sp.wait_ge(tables, 1)
            sp.dma_start(d_row[NA - 1:NA, :], D.rearrange("(a h) -> a h", a=1)).then_inc(d_in, 16)
            sp.dma_start(wr_rows[:, :], bass.AP(Wr.tensor, 0, [[P, CH], [LEN, EXPERTS], [1, P]])).then_inc(wr_in, 16)
            sp.wait_ge(px_full, 1)
            sp.dma_start(a_rows, A.rearrange("e r d -> (e r) d")).then_inc(a_in, 16)
            sp.wait_ge(b_ready, 1)
            load_w(4)
            sp.wait_ge(wt_full, w_tile(0) + 1)
            load_rows(0, 1)
            sp.wait_ge(wt_full, w_tile(2) + 1)
            load_w(6)
            load_w(7)
            sp.wait_ge(wt_full, TILE_B + 1)
            load_w(5)
            sp.wait_ge(consts, 4)
            sp.dma_start(kpad[:, LEN:KPITCH], zeros[:, :]).then_inc(pad_stored, 16)
            sp.dma_start(len_i[:, :], bass.AP(lengths.tensor, 0, [[0, P], [1, SEQS]])).then_inc(small_in, 16)
            for h in range(2):
                sp.dma_start(lang_i[h * SEQS:(h + 1) * SEQS, :],
                             languages.rearrange("(b a) -> b a", a=1)).then_inc(small_in, 16)
            store_kernels(0)
            sp.wait_ge(pad_stored, 16)
            sp.wait_ge(k_stored, 16)
            sp.wait_ge(prm_full, 2)
            for h, loaded in enumerate((toe_half, toe_in[0])):
                sp.dma_start(toe[0][:, h, :], bass.AP(kpad.tensor, h * KPITCH, [[1, P], [1, LEN]])
                             ).then_inc(loaded, 16)
            sp.wait_ge(wt_full, w_tile(5) + 1)
            load_toe(0, 1)

            def step(b, m):
                i = BODY * b + m
                sp.wait_ge(px_full, i + 1)
                load_rows(b, m + 2)
                if m + 2 >= BODY:
                    sp.wait_ge(k_stored, 16 * b + 32)
                sp.wait_ge(thi_ready, i + 1)
                sp.wait_ge(tlo_ready, i + 1)
                load_toe(b, m + 2)

            sp.wait_ge(wt_full, TILE_A + 1)
            with sp.Fori(0, LAST) as b:
                for m in range(BODY):
                    step(b, m)
                    if m == 1:
                        store_kernels(b + 1)
            for m in range(BODY - 2):
                sp.wait_ge(px_full, BODY * LAST + m + 1)
                load_rows(LAST, m + 2)
                sp.wait_ge(thi_ready, BODY * LAST + m + 1)
                sp.wait_ge(tlo_ready, BODY * LAST + m + 1)
                load_toe(LAST, m + 2)

        @block.gpsimd
        def _(pool):
            nc.gpsimd.memset(ident[:, :], 0.0).then_inc(consts, 1)
            pool.wait_ge(consts, 1)
            nc.gpsimd.affine_select(out=ident[:, :], in_=ident[:, :], compare_op=ALU.not_equal, fill=1.0,
                                    base=0, pattern=[[-1, P]], channel_multiplier=1).then_inc(ident_ready, 1)
            nc.gpsimd.iota(pos[:, 0:NB], [[-1, NB]], base=NB - 1, channel_multiplier=0,
                           allow_small_or_imprecise_dtypes=True).then_inc(consts, 1)
            nc.gpsimd.iota(pos[:, NB:POS], [[-NB, NA]], base=NB * (NA - 1), channel_multiplier=0,
                           allow_small_or_imprecise_dtypes=True).then_inc(consts, 1)
            nc.gpsimd.memset(zeros[:, :], 0.0).then_inc(consts, 1)
            nc.gpsimd.iota(sample_no[:, :], [[P, CH]], base=0, channel_multiplier=1,
                           allow_small_or_imprecise_dtypes=True).then_inc(consts, 1)
            nc.gpsimd.iota(expert_no[:, :], [[1, EXPERTS]], base=0, channel_multiplier=0,
                           allow_small_or_imprecise_dtypes=True).then_inc(consts, 1)
            for s in range(2):
                nc.gpsimd.memset(u_hi[s][:, 0:LEAD, :].bitcast(F32), 0.0).then_inc(consts, 1)
                nc.gpsimd.memset(u_lo[s][:, 0:LEAD, :].bitcast(F32), 0.0).then_inc(consts, 1)
            pool.wait_ge(consts, 6)
            pool.wait_ge(prm_ready, 1)

            def products(g):
                heads = bass.ds(g * KG, KG)
                at = pos[:, :].unsqueeze(1).to_broadcast([P, KG, POS])
                nc.gpsimd.tensor_tensor(turn[:, :, :], prm[:, 1, heads].unsqueeze(2).to_broadcast([P, KG, POS]),
                                        at, ALU.mult).then_inc(prod_ready, 1)
                nc.gpsimd.tensor_tensor(mag[:, :, :], prm[:, 0, heads].unsqueeze(2).to_broadcast([P, KG, POS]),
                                        at, ALU.mult).then_inc(prod_ready, 1)

            products(0)
            pool.wait_ge(b_in, 16)
            for e in range(EXPERTS):
                ins = nc.gpsimd.tensor_copy(b_sorted[:, :, e, :], b_rows[:, e, :, :])
            ins.then_inc(b_ready, 1)
            with pool.Fori(0, LAST) as b:
                pool.wait_ge(k_full, b + 1)
                products(b + 1)

        @block.scalar
        def _(act):
            def weight(k):
                act.wait_ge(wt_full, k + 1)
                turned, hi = tile_views(k, w_hi, bt_hi)
                nc.scalar.activation(hi, turned, ACT.Copy).then_inc(whi_ready, 1)

            def copy_parameters(k):
                act.wait_ge(prm_full, k // 2 + 1)
                nc.scalar.activation(prm[:, k:k + 2, :],
                                     pg[:, k * HEADS:(k + 2) * HEADS].rearrange("p (k h) -> p k h", k=2), ACT.Copy
                                     ).then_inc(prm_ready, 1)

            def magnitudes(g):
                act.wait_ge(prod_ready, 2 * g + 2)
                nc.scalar.activation(mag[:, :, :], mag[:, :, :], ACT.Exp).then_inc(mag_ready, 1)

            def waves(g):
                act.wait_ge(angle_ready, g + 1)
                nc.scalar.activation(wave[:, :, :], wave[:, :, :], ACT.Sin, scale=-TWO_PI, bias=phase[:, 2:3]
                                     ).then_inc(wave_ready, 1)
                nc.scalar.activation(wave2[:, :, :], wave2[:, :, :], ACT.Sin, scale=-TWO_PI, bias=phase[:, 3:4]
                                     ).then_inc(wave_ready, 1)

            def copy_kernels(g):
                act.wait_ge(k_full, g + 1)
                nc.scalar.activation(k_rows[:, :, :], k_psum, ACT.Copy).then_inc(k_copied, 1)

            def split_rows(b, m, first=False):
                i, s = BODY * b + m, m % 2
                act.wait_ge(px_full, i + 1)
                if not first:
                    act.wait_ge(ylo_ready, i - 1)
                nc.scalar.activation(xt[s][:, :, :], px[:, :, :], ACT.Copy).then_inc(xt_ready, 1)
                if not first:
                    act.wait_ge(conv_done, i - 1)
                nc.scalar.activation(u_hi[s][:, LEAD:LEAD + CH, :], px[:, :, :], ACT.Copy).then_inc(uhi_ready, 1)

            def split_toe(b, m):
                s = m % 2
                act.wait_ge(toe_in[s], 32 * b + 16 * (m // 2 + 1))
                nc.scalar.activation(t_hi[s][:, :, :], toe_f[s], ACT.Copy).then_inc(thi_ready, 1)

            def split_y(b, m):
                s = m % 2
                act.wait_ge(merged, BODY * b + m + 1)
                nc.scalar.activation(y_hi[s][:, :, :], xt[s][:, :, :], ACT.Copy).then_inc(yhi_ready, 1)

            def finish(b, m, kernels=False):
                i, s = BODY * b + m, m % 2
                act.wait_ge(router, ROUTER * i + 2)
                nc.scalar.activation(ratio[:, :], top[:, 0:1], ACT.Exp, scale=-1.0, bias=top[:, 1:2]
                                     ).then_inc(ratio_ready, 1)
                if kernels:
                    magnitudes(b + 1)
                    waves(b + 1)
                act.wait_ge(gt_full, i + 1)
                nc.scalar.activation(gt_hi[:, :], pg[:, 0:P], ACT.Copy).then_inc(gthi_ready, 1)
                act.wait_ge(proj_done, i + 1)
                act.wait_ge(result_dma[s], START + 64 * b + 32 * (m // 2))
                for n, (c0, c1) in enumerate(BANKS):
                    c1 = min(c1, LEN)
                    ins = nc.scalar.activation(result[s][:, c0:c1], pm[:, n, 0:c1 - c0], ACT.Copy)
                ins.then_inc(pm_free, 1)
                act.wait_ge(pm_free, i + 2)
                for h in range(2):
                    act.dma_start(bass.AP(out.tensor, (2 * i + h) * LEN, [[HEADS * LEN, SEQS], [1, LEN]]),
                                  result[s][h * SEQS:(h + 1) * SEQS, :]).then_inc(result_dma[s], 16)

            act.sem_inc(pm_free, 1)
            for s in range(2):
                act.sem_inc(result_dma[s], START)
            act.wait_ge(px_full, 1)
            nc.scalar.activation(xt[0][:, :, :], px[:, :, :], ACT.Copy).then_inc(xt_ready, 1)
            copy_parameters(0)
            nc.scalar.activation(tanh_half, dt_re, ACT.Tanh, scale=0.5).then_inc(par_act, 1)
            nc.scalar.activation(sin1, turns, ACT.Sin, scale=TWO_PI).then_inc(par_act, 1)
            nc.scalar.activation(sin_half, turns, ACT.Sin, scale=TWO_PI / 2).then_inc(par_act, 1)
            magnitudes(0)
            waves(0)
            nc.scalar.activation(u_hi[0][:, LEAD:LEAD + CH, :], px[:, :, :], ACT.Copy).then_inc(uhi_ready, 1)
            copy_parameters(2)
            for k in range(2):
                weight(k)
            copy_kernels(0)
            for k in range(2, X1_TURN):
                weight(k)
            split_rows(0, 1, first=True)
            for h, (loaded, half) in enumerate(((toe_half, thi_half), (toe_in[0], thi_ready))):
                act.wait_ge(loaded, 16)
                nc.scalar.activation(t_hi[0][:, h, :], toe_f[0][:, h, :], ACT.Copy).then_inc(half, 1)
            for k in range(X1_TURN, WTILES):
                weight(k)
            split_toe(0, 1)
            split_y(0, 0)

            def step(b, m, rows_left=True, kernels=True):
                if rows_left:
                    act.wait_ge(conv_done, BODY * b + m + 1)
                    split_toe(b, m + 2)
                    split_rows(b, m + 2)
                split_y(b, m + 1)
                if kernels and m == 1:
                    copy_kernels(b + 1)
                finish(b, m, kernels and m == 0)

            with act.Fori(0, LAST) as b:
                for m in range(BODY):
                    step(b, m)
            for m in range(BODY - 1):
                step(LAST, m, rows_left=m < BODY - 2, kernels=False)
            finish(LAST, BODY - 1)
            for s in range(2):
                act.wait_ge(result_dma[s], START + 16 * PAIRS)

        @block.vector
        def _(dve):
            n_par = [0]

            def par_step(ins, behind=0):
                n_par[0] += 1
                ins.then_inc(par_dve, 1)
                dve.wait_ge(par_dve, n_par[0] - behind)

            vec = nc.vector
            vec.memset(d_row[:, :], 0.0)
            vec.memset(phase[0:HEADS, 0:1], 0.25)
            vec.memset(phase[HEADS:P, 0:1], 0.0)
            vec.memset(phase[0:HEADS, 1:2], 0.0)
            vec.memset(phase[HEADS:P, 1:2], 0.25).then_inc(tables, 1)
            dve.wait_ge(tables, 1)
            vec.tensor_scalar(phase[:, 2:4], phase[:, 0:2], TWO_PI, None, ALU.mult).then_inc(tables, 1)

            def angles(g):
                far = turn[:, :, NB:POS]
                dve.wait_ge(prod_ready, 2 * g + 1)
                vec.tensor_scalar(wave[:, :, :], turn[:, :, :], phase[:, 0:1], MAGIC, ALU.add, ALU.add
                                  ).then_inc(angle_step, 1)
                vec.tensor_scalar(wave2[:, :, :], far, phase[:, 1:2], MAGIC, ALU.add, ALU.add).then_inc(angle_step, 1)
                dve.wait_ge(angle_step, 2 * g + 2)
                vec.scalar_tensor_tensor(out=wave[:, :, :], in0=wave[:, :, :], scalar=MAGIC, in1=turn[:, :, :],
                                         op0=ALU.subtract, op1=ALU.subtract)
                vec.scalar_tensor_tensor(out=wave2[:, :, :], in0=wave2[:, :, :], scalar=MAGIC, in1=far,
                                         op0=ALU.subtract, op1=ALU.subtract).then_inc(angle_ready, 1)

            def exact_exp(out, x, n, behind):
                k, q, two_k = ex_k[:, 0:n], ex_q[:, 0:n], ex_2k[:, 0:n]
                yield par_step(vec.tensor_scalar(k, x, 1.0 / math.log(2.0), MAGIC, ALU.mult, ALU.add), behind)
                yield par_step(vec.tensor_scalar(k, k, MAGIC, -126.0, ALU.subtract, ALU.max), behind)
                yield par_step(vec.tensor_scalar(k, k, 127.0, None, ALU.min), behind)
                yield par_step(vec.scalar_tensor_tensor(out=out, in0=k, scalar=-LN2_HI, in1=x,
                                                        op0=ALU.mult, op1=ALU.add), behind)
                yield par_step(vec.scalar_tensor_tensor(out=out, in0=k, scalar=-LN2_LO, in1=out,
                                                        op0=ALU.mult, op1=ALU.add), behind)
                yield par_step(vec.tensor_scalar(q, out, 1.0 / math.factorial(7), None, ALU.mult), behind)
                for m in range(6, 0, -1):
                    yield par_step(vec.scalar_tensor_tensor(out=q, in0=q, scalar=1.0 / math.factorial(m), in1=out,
                                                            op0=ALU.add, op1=ALU.mult), behind)
                yield par_step(vec.tensor_scalar(two_k, k, 127.0, 2.0 ** 23, ALU.add, ALU.mult), behind)
                yield par_step(vec.scalar_tensor_tensor(out=out, in0=q, scalar=1.0, in1=two_k.bitcast(F32),
                                                        op0=ALU.add, op1=ALU.mult), behind)

            dve.wait_ge(logs_in, 32)
            for _ in exact_exp(exps[:, :], logs[:, :], MODES + 1, 0):
                pass
            dve.wait_ge(par_in, 32)
            par_step(vec.tensor_scalar(dt_im, a_im, step_h[:, :], None, ALU.mult), 1)
            par_step(vec.tensor_scalar(dt_re, a_re, step_h[:, :], -1.0, ALU.mult, ALU.mult), 1)
            decay_exp = exact_exp(expo, dt_re, MODES, 1)
            par_step(vec.tensor_scalar(revs, dt_im, 1.0 / (2.0 * math.pi), None, ALU.mult), 1)
            next(decay_exp)
            par_step(vec.tensor_scalar(whole, revs, MAGIC, None, ALU.add), 1)
            next(decay_exp)
            par_step(vec.tensor_scalar(whole, whole, MAGIC, None, ALU.subtract), 1)
            next(decay_exp)
            par_step(vec.tensor_tensor(par[:, 1, halves[0]], revs, whole, ALU.subtract), 1)
            par_step(vec.tensor_tensor(par[:, 1, halves[1]], revs, whole, ALU.subtract), 1)
            par_step(vec.tensor_scalar(par[:, 0, halves[1]], dt_re, 1.0, None, ALU.mult), 0)
            assert n_par[0] == A_STEPS
            next(decay_exp)
            par_step(vec.tensor_tensor(t1, a_re, a_re, ALU.mult), 1)
            next(decay_exp)
            par_step(vec.tensor_tensor(t2, a_im, a_im, ALU.mult), 1)
            next(decay_exp)
            par_step(vec.tensor_tensor(norm, t1, t2, ALU.add), 1)
            next(decay_exp)
            par_step(vec.reciprocal(norm, norm), 1)
            next(decay_exp)
            par_step(vec.scalar_tensor_tensor(out=n_re, in0=a_re, scalar=-2.0, in1=norm, op0=ALU.mult, op1=ALU.mult), 1)
            next(decay_exp)
            par_step(vec.scalar_tensor_tensor(out=n_im, in0=a_im, scalar=-2.0, in1=norm, op0=ALU.mult, op1=ALU.mult), 1)
            next(decay_exp)
            c_re, c_im = c_in[:, :, 0], c_in[:, :, 1]
            par_step(vec.tensor_tensor(t1, c_re, n_re, ALU.mult), 1)
            next(decay_exp)
            par_step(vec.tensor_tensor(t2, c_im, n_im, ALU.mult), 1)
            next(decay_exp)
            par_step(vec.tensor_tensor(t3, c_re, n_im, ALU.mult), 1)
            next(decay_exp)
            par_step(vec.tensor_tensor(t4, c_im, n_re, ALU.mult), 1)
            next(decay_exp)
            par_step(vec.tensor_tensor(g_re, t1, t2, ALU.subtract), 1)
            par_step(vec.tensor_tensor(g_im, t3, t4, ALU.add), 1)
            angles(0)
            dve.wait_ge(par_act, 3)
            par_step(vec.scalar_tensor_tensor(out=em1, in0=expo, scalar=1.0, in1=tanh_half, op0=ALU.add, op1=ALU.mult), 1)
            par_step(vec.scalar_tensor_tensor(out=cos1, in0=sin_half, scalar=-2.0, in1=sin_half,
                                              op0=ALU.mult, op1=ALU.mult), 0)
            par_step(vec.scalar_tensor_tensor(out=t1, in0=cos1, scalar=1.0, in1=em1, op0=ALU.add, op1=ALU.mult), 1)
            par_step(vec.tensor_tensor(e_im, expo, sin1, ALU.mult), 1)
            par_step(vec.tensor_tensor(e_re, t1, cos1, ALU.add), 1)
            par_step(vec.tensor_tensor(t2, g_im, e_im, ALU.mult), 1)
            par_step(vec.tensor_tensor(t1, g_re, e_re, ALU.mult), 1)
            par_step(vec.tensor_tensor(t3, g_re, e_im, ALU.mult), 1)
            par_step(vec.tensor_tensor(t4, g_im, e_re, ALU.mult), 1)
            par_step(vec.tensor_tensor(par[:, 2, halves[0]], t1, t2, ALU.subtract), 1)
            par_step(vec.tensor_tensor(par[:, 2, halves[1]], t2, t1, ALU.subtract), 1)
            for half in halves:
                par_step(vec.scalar_tensor_tensor(out=par[:, 3, half], in0=t3, scalar=-1.0, in1=t4,
                                                  op0=ALU.mult, op1=ALU.subtract), 1)
            assert n_par[0] == PAR_STEPS

            def low_weight(k):
                dve.wait_ge(whi_ready, k + 1)
                turned, hi = tile_views(k, w_hi, bt_hi)
                vec.tensor_tensor(tile_views(k, w_lo, bt_lo)[1], turned, hi.bitcast(F32), ALU.subtract
                                  ).then_inc(wlo_ready, 1)

            def factors(g):
                heads = bass.ds(g * KG, KG)
                far = wave[:, :, NB:POS]
                dve.wait_ge(wave_ready, 2 * g + 2)
                dve.wait_ge(mag_ready, g + 1)
                vec.tensor_tensor(far, far, prm[:, 2, heads].unsqueeze(2).to_broadcast([P, KG, NA]), ALU.mult
                                  ).then_inc(fac_step, 1)
                vec.tensor_tensor(wave2[:, :, :], wave2[:, :, :],
                                  prm[:, 3, heads].unsqueeze(2).to_broadcast([P, KG, NA]), ALU.mult
                                  ).then_inc(fac_step, 1)
                dve.wait_ge(fac_step, 3 * g + 2)
                vec.tensor_tensor(far, far, wave2[:, :, :], ALU.add).then_inc(fac_step, 1)
                dve.wait_ge(fac_step, 3 * g + 3)
                vec.tensor_tensor(wave[:, :, :], wave[:, :, :], mag[:, :, :], ALU.mult).then_inc(fac_ready, 1)

            def first_samples(g):
                dve.wait_ge(k_copied, g + 1)
                at0 = k_rows[:, :, NB - 1:NB].rearrange("p h q -> p (h q)")
                vec.tensor_tensor(at0, at0, d_one[:, bass.ds(g * KG, KG)], ALU.add).then_inc(k_ready, 1)

            def split_rows(b, m, first=False):
                i, s = BODY * b + m, m % 2
                dve.wait_ge(xt_ready, i + 1)
                dve.wait_ge(uhi_ready, i + 1)
                if not first:
                    dve.wait_ge(conv_done, i - 1)
                at = slice(LEAD, LEAD + CH)
                vec.tensor_tensor(u_lo[s][:, at, :], xt[s][:, :, :], u_hi[s][:, at, :].bitcast(F32), ALU.subtract
                                  ).then_inc(ulo_ready, 1)

            def split_toe(b, m):
                s = m % 2
                dve.wait_ge(thi_ready, BODY * b + m + 1)
                vec.tensor_tensor(t_lo[s][:, :, :], toe_f[s], t_hi[s][:, :, :].bitcast(F32), ALU.subtract
                                  ).then_inc(tlo_ready, 1)

            def hold():
                vec.tensor_copy(held[:, :], lang_f[:, :])

            def merge(b, m):
                i, s = BODY * b + m, m % 2
                dve.wait_ge(ulo_ready, i + 1)
                dve.wait_ge(conv_done, i + 1)
                hold()
                for h in range(2):
                    ins = vec.copy_predicated(xt[s][:, :, h * SEQS:(h + 1) * SEQS], valid[:, :, :], pc[:, h, :, :])
                ins.then_inc(merged, 1)
                dve.wait_ge(yhi_ready, i + 1)
                vec.tensor_tensor(y_lo[s][:, :, :], xt[s][:, :, :], y_hi[s][:, :, :].bitcast(F32), ALU.subtract
                                  ).then_inc(ylo_ready, 1)

            def route(b, m):
                i = BODY * b + m
                gate = pm[:, 2, :]
                base = ROUTER * i
                dve.wait_ge(gate_done, i + 1)
                vec.tensor_tensor(logits[:, :], gate[:, L0:L0 + EXPERTS], bias[:, :], ALU.add).then_inc(router, 1)
                dve.wait_ge(router, base + 1)
                hold()
                vec.max(top[:, :], logits[:, :]).then_inc(router, 1)
                dve.wait_ge(router, base + 2)
                hold()
                vec.max_index(top_at[:, :], top[:, :], logits[:, :]).then_inc(router, 1)
                dve.wait_ge(router, base + 3)
                vec.tensor_copy(top_no[:, :], top_at[:, 0:2]).then_inc(router, 1)
                dve.wait_ge(ratio_ready, i + 1)
                vec.tensor_scalar(half_sum[:, :], ratio[:, :], 1.0 / SCALING, 1.0 / SCALING, ALU.mult, ALU.add
                                  ).then_inc(router, 1)
                dve.wait_ge(router, base + 5)
                vec.reciprocal(weight[:, 0:1], half_sum[:, :]).then_inc(router, 1)
                dve.wait_ge(router, base + 6)
                vec.tensor_tensor(weight[:, 1:2], weight[:, 0:1], ratio[:, :], ALU.mult).then_inc(router, 1)
                vec.tensor_scalar(gate1[:, :], expert_no[:, :], top_no[:, 0:1], weight[:, 0:1],
                                  ALU.is_equal, ALU.mult)
                dve.wait_ge(router, base + 7)
                vec.tensor_scalar(gate2[:, :], expert_no[:, :], top_no[:, 1:2], weight[:, 1:2],
                                  ALU.is_equal, ALU.mult).then_inc(router, 1)
                dve.wait_ge(router, base + 8)
                vec.tensor_tensor(gates[:, :], gate1[:, :], gate2[:, :], ALU.add).then_inc(router, 1)
                dve.wait_ge(router, base + 9)
                vec.tensor_tensor(gated[:, :, :], gate[:, H0:L0].rearrange("p (e r) -> p e r", e=EXPERTS),
                                  gates[:, :].unsqueeze(2).to_broadcast([P, EXPERTS, RANK]), ALU.mult
                                  ).then_inc(gated_ready, 1)
                dve.wait_ge(gthi_ready, i + 1)
                vec.tensor_tensor(gt_lo[:, :], pg[:, 0:P], gt_hi[:, :].bitcast(F32), ALU.subtract
                                  ).then_inc(gtlo_ready, 1)

            dve.wait_ge(d_in, 16)
            dve.wait_ge(ident_ready, 1)
            vec.tensor_scalar(d_one[:, :], d_row[:, :], ident[0:NA, NA - 1:NA], None, ALU.add).then_inc(tables, 1)
            dve.wait_ge(prm_ready, 2)
            factors(0)
            for k in range(2):
                low_weight(k)
            dve.wait_ge(tables, 3)
            first_samples(0)
            split_rows(0, 0, first=True)
            for k in range(2, X1_TURN):
                low_weight(k)
            for h, (hi, lo) in enumerate(((thi_half, tlo_half), (thi_ready, tlo_ready))):
                if h == 1:
                    split_rows(0, 1, first=True)
                dve.wait_ge(hi, 1)
                vec.tensor_tensor(t_lo[0][:, h, :], toe_f[0][:, h, :], t_hi[0][:, h, :].bitcast(F32), ALU.subtract
                                  ).then_inc(lo, 1)
            for k in range(X1_TURN, WTILES):
                low_weight(k)
            split_toe(0, 1)
            dve.wait_ge(small_in, 48)
            dve.wait_ge(consts, 6)
            vec.tensor_copy(len_f[:, :], len_i[:, :]).then_inc(tables, 1)
            vec.tensor_copy(lang_f[:, :], lang_i[:, :]).then_inc(tables, 1)
            dve.wait_ge(tables, 5)
            vec.tensor_tensor(valid[:, :, :], sample_no[:, :].unsqueeze(2).to_broadcast([P, CH, SEQS]),
                              len_f[:, :].unsqueeze(1).to_broadcast([P, CH, SEQS]), ALU.is_lt).then_inc(tables, 1)
            vec.tensor_scalar(bias[:, :], expert_no[:, :], lang_f[:, :], LANG_BIAS, ALU.is_equal, ALU.mult
                              ).then_inc(tables, 1)
            dve.wait_ge(tables, TABLES)
            merge(0, 0)

            def step(b, m, rows_left=True, kernels=True):
                if kernels and m == 0:
                    angles(b + 1)
                if kernels and m == 1:
                    factors(b + 1)
                if rows_left:
                    split_toe(b, m + 2)
                    split_rows(b, m + 2)
                merge(b, m + 1)
                if kernels and m == 1:
                    first_samples(b + 1)
                route(b, m)

            with dve.Fori(0, LAST) as b:
                for m in range(BODY):
                    step(b, m)
            for m in range(BODY - 1):
                step(LAST, m, rows_left=m < BODY - 2, kernels=False)
            route(LAST, BODY - 1)

        @block.tensor
        def _(pe):
            pe.wait_ge(ident_ready, 1)

            def turn_weight(k):
                what, place, at = TILE[k]
                loaded, staged = {W_: (w_in[at.start // P], w_rows[at.start // P]) if what == W_ else None,
                                  A_: (a_in, a_rows), WR_: (wr_in, wr_rows), B_: (b_ready, b_sorted)}[what]
                pe.wait_ge(loaded, 1 if what == B_ else 16)
                before = [j for j in range(k) if TILE[j][1] is place]
                if before:
                    pe.wait_ge(wlo_ready, before[-1] + 1)
                if what == A_:
                    pe.wait_ge(k_copied, 1)
                if place is in_px:
                    pe.wait_ge(uhi_ready, 1 if k < X1_TURN else 2)
                if what == WR_:
                    place = place.rearrange("p c o -> p (c o)")
                    nc.tensor.transpose(place[:, 0:CH * EXPERTS], staged[:, :], ident[0:CH * EXPERTS, 0:CH * EXPERTS]
                                        ).then_inc(wt_full, 1)
                    return
                for c in range(CH):
                    chunk = (staged[:, c, :, :].rearrange("p e r -> p (e r)") if what == B_
                             else staged[:, c * P:(c + 1) * P])
                    ins = nc.tensor.matmul(place[:, c, :], chunk, ident[:, :], is_transpose=True,
                                           start=c % 4 == 0, stop=True, skip_group_check=True)
                if what == W_:
                    ins = nc.tensor.matmul(place[:, at.start // P, :], ident[:, :], ident[:, :], start=False, stop=True,
                                           skip_group_check=True)
                ins.then_inc(wt_full, 1)

            def turn_parameters(k):
                for n in (k, k + 1):
                    ins = nc.tensor.transpose(pg[:, n * HEADS:(n + 1) * HEADS], par[:, n, :],
                                              ident[0:HEADS, 0:HEADS])
                ins.then_inc(prm_full, 1)

            def make_kernels(g):
                pe.wait_ge(fac_ready, g + 1)
                for h in range(KG):
                    ins = nc.tensor.matmul(k_psum[:, h, :], wave[:, h, NB:POS], wave[:, h, 0:NB],
                                           start=True, stop=True)
                ins.then_inc(k_full, 1)

            def turn_rows(b, m, first=False):
                i, s = BODY * b + m, m % 2
                pe.wait_ge(rows_in[s], 64 * b + 32 * (m // 2 + 1))
                if not first:
                    pe.wait_ge(uhi_ready, i)
                for c in range(CH):
                    ins = nc.tensor.transpose(px[:, c, :], rows[s][:, c * P:(c + 1) * P], ident[:, :])
                ins.then_inc(px_full, 1)

            def convolve(b, m, first=False):
                i, s = BODY * b + m, m % 2
                pe.wait_ge(uhi_ready, i + 1)
                pe.wait_ge(ulo_ready, i + 1)
                if first:
                    pe.wait_ge(thi_half, 1)
                    pe.wait_ge(tlo_half, 1)
                    pe.wait_ge(consts, 10)
                    pe.wait_ge(wlo_ready, w_tile(5) + 1)
                else:
                    pe.wait_ge(thi_ready, i + 1)
                    pe.wait_ge(tlo_ready, i + 1)
                    pe.wait_ge(merged, i)
                for h in range(2):
                    if first and h == 1:
                        pe.wait_ge(thi_ready, 1)
                        pe.wait_ge(tlo_ready, 1)
                    tok = slice(h * SEQS, (h + 1) * SEQS)
                    for d in range(CH):
                        lead = max(0, d - (CH - 1 - LEAD))
                        n = CH - d + lead
                        for t, u in ((t_hi, u_hi), (t_hi, u_lo), (t_lo, u_hi)):
                            ins = nc.tensor.matmul(pc[:, h, CH - n:CH, :], t[s][:, h, d * P:(d + 1) * P],
                                                   u[s][:, LEAD - lead:LEAD - lead + n, tok],
                                                   start=(d == 0 and u is u_hi and t is t_hi),
                                                   stop=(d == CH - 1 and t is t_lo))
                ins.then_inc(conv_done, 1)

            def project(b, m):
                i, s = BODY * b + m, m % 2
                pe.wait_ge(yhi_ready, i + 1)
                pe.wait_ge(ylo_ready, i + 1)
                pe.wait_ge(pm_free, i + 1)
                for n in (2, 0, 1):
                    c0, c1 = BANKS[n]
                    for c in range(CH):
                        if n == 1 and c == CH // 2:
                            pe.wait_ge(gated_ready, i + 1)
                            if m == 1:
                                pe.wait_ge(k_copied, b + 2 if b is not LAST else KGROUPS)
                            nc.tensor.transpose(pg[:, 0:P], gated[:, :, :].rearrange("p e r -> p (e r)"), ident[:, :]
                                                ).then_inc(gt_full, 1)
                        for y, w in ((y_hi, w_hi), (y_lo, w_hi), (y_hi, w_lo)):
                            ins = nc.tensor.matmul(pm[:, n, 0:c1 - c0], y[s][:, c, :], w[:, c, c0:c1],
                                                   start=(c == 0 and y is y_hi and w is w_hi),
                                                   stop=(c == CH - 1 and w is w_lo), skip_group_check=True)
                    if n == 2:
                        ins.then_inc(gate_done, 1)
                pe.wait_ge(gthi_ready, i + 1)
                pe.wait_ge(gtlo_ready, i + 1)
                for n, (c0, c1) in enumerate(BANKS):
                    c1 = min(c1, LEN)
                    for g, w in ((gt_hi, bt_hi), (gt_lo, bt_hi), (gt_hi, bt_lo)):
                        ins = nc.tensor.matmul(pm[:, n, 0:c1 - c0], g[:, :], w[:, c0:c1], start=False,
                                               stop=w is bt_lo, skip_group_check=True)
                ins.then_inc(proj_done, 1)

            turn_rows(0, 0, first=True)
            pe.wait_ge(par_dve, A_STEPS)
            turn_parameters(0)
            for k in range(2):
                turn_weight(k)
            pe.wait_ge(par_dve, PAR_STEPS)
            turn_parameters(2)
            for k in range(2, 4):
                turn_weight(k)
            pe.wait_ge(prm_ready, 2)
            make_kernels(0)
            for k in range(4, X1_TURN):
                turn_weight(k)
            pe.wait_ge(wlo_ready, w_tile(4) + 1)
            turn_rows(0, 1)
            for k in range(X1_TURN, WTILES):
                turn_weight(k)
            convolve(0, 0, first=True)
            pe.wait_ge(wlo_ready, WTILES)

            def step(b, m, rows_left=True, kernels=True):
                if rows_left:
                    turn_rows(b, m + 2)
                convolve(b, m + 1)
                if kernels and m == 1:
                    make_kernels(b + 1)
                project(b, m)

            with pe.Fori(0, LAST) as b:
                for m in range(BODY):
                    step(b, m)
            for m in range(BODY - 1):
                step(LAST, m, rows_left=m < BODY - 2, kernels=False)
            project(LAST, BODY - 1)


_INS = ["x", "itok_B_8_3872", "itok_B_0_7", "L0_cond_log_dt", "L0_cond_C", "L0_cond_log_A_real", "L0_cond_A_imag",
        "L0_cond_D", "L1_cond_W", "L1_cond_Wr", "L1_cond_A", "L1_cond_B"]


def kernel(**inputs):
    import numpy as _np
    import concourse.bacc as _bacc
    from concourse import mybir as _mybir
    from concourse.bass_utils import run_bass_kernel_spmd as _run

    nc = _bacc.Bacc("TRN2", target_bir_lowering=False, num_devices=1)
    arrays, args = {}, []
    for name in _INS:
        a = _np.ascontiguousarray(inputs[name])
        arrays[f"in_{name}"] = a
        args.append(nc.dram_tensor(f"in_{name}", a.shape, _mybir.dt.from_np(a.dtype), kind="ExternalInput").ap())
    args.append(nc.dram_tensor("out_0", (SEQS, HEADS, LEN), _mybir.dt.float32, kind="ExternalOutput").ap())
    cond_resid_kernel(nc, *args)
    r = _run(nc, [arrays], core_ids=[0])
    return r.results[0]["out_0"]
```

```python
import math
from contextlib import ExitStack

import concourse.bass as bass
from concourse import mybir

F32 = mybir.dt.float32
F32R = mybir.dt.float32r
I32 = mybir.dt.int32
U32 = mybir.dt.uint32
ALU = mybir.AluOpType
ACT = mybir.ActivationFunctionType

P = 128
SEQS, HEADS, LEN = 64, 64, 1024
MODES = 64
CH = LEN // P
PAIRS = HEADS // 2
FAR = 5
EXPERTS, RANK = 8, 16
ER = EXPERTS * RANK
LANG_BIAS, SCALING = 5.0, 2.0
WCOLS = LEN + ER + EXPERTS
BANKS = [(0, 388), (388, 776), (776, WCOLS)]
BANK_ORDER = (2, 0, 1)
GATE = BANKS[2]
H0 = LEN - GATE[0]
L0 = H0 + ER
KPITCH = LEN + P

NA, NB = 16, 64
POS = NB + NA
KG = 8
KGROUPS = HEADS // KG
MAGIC = 1.5 * 2.0 ** 23
LN2_HI, LN2_LO = 0.693359375, -2.12194440054690583e-4
TWO_PI = 6.283185


def cond_resid_kernel(nc, x, lengths, languages, log_dt, C, log_A_real, A_imag, D, W, Wr, A, B, out):
    kpad = nc.dram_tensor("kpad", (HEADS, KPITCH), F32, kind="Internal").ap()
    with ExitStack() as ctx:
        def sb(name, shape, dt=F32):
            return ctx.enter_context(nc.sbuf_tensor(name, shape, dt))

        def pb(name, shape):
            return ctx.enter_context(nc.psum_tensor(name, shape, F32))

        def sem(name):
            return ctx.enter_context(nc.semaphore(name))

        w_hi = sb("w_hi", [P, CH, WCOLS], F32R)
        w_lo = sb("w_lo", [P, CH, WCOLS], F32R)
        bt_hi = sb("bt_hi", [P, LEN], F32R)
        bt_lo = sb("bt_lo", [P, LEN], F32R)
        valid = sb("valid", [P, CH, SEQS], I32)
        bias = sb("bias", [P, EXPERTS])
        ident = sb("ident", [P, P])
        expert_no = sb("expert_no", [P, EXPERTS])
        rows = [sb(f"rows{s}", [P, LEN]) for s in range(2)]
        xt = [sb(f"xt{s}", [P, CH, P]) for s in range(2)]
        u = [sb(f"u{s}", [P, 2, CH, P], F32R) for s in range(2)]
        u_hi, u_lo = [[t[:, q, :, :] for t in u] for q in range(2)]
        toe = [sb(f"toe{s}", [P, 2, LEN]) for s in range(2)]
        toe_f = [bass.AP(t[:, :, :].tensor, LEN - 1, [[2 * LEN, P], [LEN, 2], [-1, LEN]]) for t in toe]
        t_hi = [sb(f"t_hi{s}", [P, 2, LEN], F32R) for s in range(2)]
        t_lo = [sb(f"t_lo{s}", [P, 2, LEN], F32R) for s in range(2)]
        y_hi = [sb(f"y_hi{s}", [P, CH, P], F32R) for s in range(2)]
        y_lo = [sb(f"y_lo{s}", [P, CH, P], F32R) for s in range(2)]
        result = [sb(f"result{s}", [P, LEN]) for s in range(2)]
        far_sum = sb("far_sum", [P, 2, CH - FAR, SEQS])
        logits = sb("logits", [P, EXPERTS])
        top = sb("top", [P, 8])
        top_at = sb("top_at", [P, 8], U32)
        top_no = sb("top_no", [P, 2])
        held = sb("held", [P, 1])
        ratio = sb("ratio", [P, 1])
        half_sum = sb("half_sum", [P, 1])
        weight = sb("weight", [P, 2])
        gate1 = sb("gate1", [P, EXPERTS])
        gate2 = sb("gate2", [P, EXPERTS])
        gates = sb("gates", [P, EXPERTS])
        gated = sb("gated", [P, EXPERTS, RANK])
        gt_hi = sb("gt_hi", [P, P], F32R)
        gt_lo = sb("gt_lo", [P, P], F32R)
        mag = sb("mag", [P, KG, POS])
        turn = sb("turn", [P, KG, POS])
        wave = sb("wave", [P, KG, POS])
        wave2 = sb("wave2", [P, KG, NA])
        k_rows = sb("k_rows", [NA, KG, NB])
        prm = sb("prm", [P, 4, HEADS])
        pos = sb("pos", [P, POS])
        phase = sb("phase", [P, 4])
        d_row = sb("d_row", [NA, HEADS])
        d_one = sb("d_one", [NA, HEADS])
        logs = sb("logs", [HEADS, MODES + 1])
        exps = sb("exps", [HEADS, MODES + 1])
        ex_k = sb("ex_k", [HEADS, MODES + 1])
        ex_q = sb("ex_q", [HEADS, MODES + 1])
        ex_2k = sb("ex_2k", [HEADS, MODES + 1], I32)
        zeros = sb("zeros", [HEADS, P])
        len_i = sb("len_i", [P, SEQS], I32)
        len_f = sb("len_f", [P, SEQS])
        lang_i = sb("lang_i", [P, 1], I32)
        lang_f = sb("lang_f", [P, 1])
        sample_no = sb("sample_no", [P, CH])
        wr_rows = sb("wr_rows", [CH * EXPERTS, P])
        half1 = [toe[1][:, h, :] for h in range(2)]
        b_rows = half1[0].rearrange("p (e o r) -> p e o r", e=EXPERTS, o=8)
        b_sorted = half1[1].rearrange("p (o e r) -> p o e r", o=8, e=EXPERTS)
        xt1_rows = xt[1][:, :, :].rearrange("p c t -> p (c t)")
        w_rows = [rows[1][:, :], result[0][:, :], result[1][:, :], xt1_rows] + half1 + [rows[0][:, :], result[1][:, :]]
        a_rows = result[0][:, :]
        flat0 = toe[0][:, :, :].rearrange("p a b -> p (a b)")
        (a_im, dt_im, revs, whole, sin1, sin_half, expo, tanh_half, em1, cos1, e_re, e_im, norm, n_re, n_im, g_re,
         g_im, t1, t2, t3, t4) = [flat0[0:HEADS, n * MODES:(n + 1) * MODES] for n in range(21)]
        par = flat0[0:HEADS, 21 * MODES:29 * MODES].rearrange("h (k q) -> h k q", k=4)
        c_in = flat0[0:HEADS, 29 * MODES:31 * MODES].rearrange("h (n c) -> h n c", c=2)
        halves = (slice(0, MODES), slice(MODES, P))
        dt_re, turns = par[:, 0, 0:MODES], par[:, 1, 0:MODES]
        a_re, step_h = exps[:, 0:MODES], exps[:, MODES:MODES + 1]

        px = pb("px", [P, CH, P])
        pc = pb("pc", [P, 2, CH, SEQS])
        pmg = pb("pmg", [P, 4, 512])
        pm = pmg[:, 0:3, :]
        pg = pmg[:, 3, :]
        k_psum = pg[0:NA, :].rearrange("a (h b) -> a h b", h=KG)
        in_pc = pc[:, :, :, :].rearrange("p h c b -> p (h c b)").rearrange("p (c o) -> p c o", c=CH)
        in_pm = pm[:, 0:2, :].rearrange("p n f -> p (n f)").rearrange("p (c o) -> p c o", c=CH)
        in_pg = pmg[:, 2:4, :].rearrange("p n f -> p (n f)").rearrange("p (c o) -> p c o", c=CH)
        in_px = px[:, :, :]
        W_, A_, WR_, B_ = range(4)
        places = [(W_, in_pc), (W_, in_pm), (B_, in_px), (WR_, in_pg), (W_, in_pc), (W_, in_pm),
                  (W_, in_pg), (W_, in_pc), (W_, in_pm), (A_, in_pm), (W_, in_pg)]
        TILE = []
        for what, place in places:
            c0 = {W_: P * sum(t[0] == W_ for t in TILE), A_: LEN, WR_: LEN + ER, B_: 0}[what]
            TILE.append((what, place, slice(c0, c0 + (EXPERTS if what == WR_ else P))))
        X1_TURN = 8
        LATE = 9

        def w_tile(n):
            return [k for k, t in enumerate(TILE) if t[0] == W_][n]

        px_far = px[:, :, :].rearrange("p (h c) t -> p h (c t)", h=2)[:, :, 0:2 * (CH - FAR) * SEQS].rearrange(
            "p h (q c b) -> p h q c b", q=2, c=CH - FAR)
        pc_far = pc[:, :, FAR:CH, :]

        def tile_views(k, wide, narrow):
            what, place, at = TILE[k]
            if what == B_:
                return place, narrow[:, :].rearrange("e (p o) -> e o p", o=8)
            if what == WR_:
                place = place.rearrange("p c o -> p (c o)")[:, 0:CH * EXPERTS].rearrange("p (c e) -> p c e", c=CH)
            return place, wide[:, :, at]

        rows_in = [sem(f"rows_in{s}") for s in range(2)]
        toe_part = [sem(f"toe_part{n}") for n in range(2)]
        toe_in = [sem(f"toe_in{s}") for s in range(2)]
        result_dma = [sem(f"result_dma{s}") for s in range(2)]
        px_full = sem("px_full")
        xt_ready = sem("xt_ready")
        uhi_ready = sem("uhi_ready")
        ulo_ready = sem("ulo_ready")
        thi_ready = sem("thi_ready")
        tlo_ready = sem("tlo_ready")
        conv_done = sem("conv_done")
        far_copied = sem("far_copied")
        far_added = sem("far_added")
        merged = sem("merged")
        yhi_ready = sem("yhi_ready")
        ylo_ready = sem("ylo_ready")
        gate_done = sem("gate_done")
        router = sem("router")
        ratio_ready = sem("ratio_ready")
        gated_ready = sem("gated_ready")
        gt_full = sem("gt_full")
        gthi_ready = sem("gthi_ready")
        gtlo_ready = sem("gtlo_ready")
        proj_done = sem("proj_done")
        pm_free = sem("pm_free")
        wt_full = sem("wt_full")
        whi_ready = sem("whi_ready")
        wlo_ready = sem("wlo_ready")
        w_in = [sem(f"w_in{n}") for n in range(CH)]
        a_in, b_in, wr_in = sem("a_in"), sem("b_in"), sem("wr_in")
        b_ready = sem("b_ready")
        thi_part, tlo_part = sem("thi_part"), sem("tlo_part")
        logs_in, par_in, d_in, small_in = sem("logs_in"), sem("par_in"), sem("d_in"), sem("small_in")
        ident_ready = sem("ident_ready")
        consts = sem("consts")
        masks = sem("masks")
        tables = sem("tables")
        par_act = sem("par_act")
        par_dve = sem("par_dve")
        prm_full, prm_ready = sem("prm_full"), sem("prm_ready")
        prod_ready = sem("prod_ready")
        angle_step = sem("angle_step")
        angle_ready = sem("angle_ready")
        mag_ready, wave_ready = sem("mag_ready"), sem("wave_ready")
        fac_step, fac_ready = sem("fac_step"), sem("fac_ready")
        k_full, k_copied, k_ready, k_stored = sem("k_full"), sem("k_copied"), sem("k_ready"), sem("k_stored")
        pad_stored = sem("pad_stored")

        block = ctx.enter_context(nc.Block())
        BODY = KG // 2
        LAST = PAIRS // BODY - 1
        WTILES = len(TILE)
        PARTS = [(0, slice(0, LEN // 2)), (0, slice(LEN // 2, LEN)), (1, slice(0, LEN))]
        TILE_B = [t[0] for t in TILE].index(B_)
        START = 16
        ROUTER = 9
        A_STEPS = 25
        PAR_STEPS = 61

        @block.sync
        def _(sp):
            sp.dma_start(logs[:, MODES:MODES + 1], log_dt.rearrange("(h a) -> h a", a=1)).then_inc(logs_in, 16)
            sp.dma_start(logs[:, 0:MODES], log_A_real).then_inc(logs_in, 16)
            sp.dma_start(a_im, A_imag).then_inc(par_in, 16)
            sp.dma_start(c_in, C).then_inc(par_in, 16)
            def load_rows(b, m):
                i, s = BODY * b + m, m % 2
                for h in range(2):
                    sp.dma_start(rows[s][h * SEQS:(h + 1) * SEQS, :],
                                 bass.AP(x.tensor, (2 * i + h) * LEN, [[HEADS * LEN, SEQS], [1, LEN]])
                                 ).then_inc(rows_in[s], 16)

            def load_toe(b, m):
                i, s = BODY * b + m, m % 2
                sp.dma_start(toe[s][:, :, :],
                             bass.AP(kpad.tensor, i * (2 * KPITCH), [[1, P], [KPITCH, 2], [1, LEN]])
                             ).then_inc(toe_in[s], 16)

            def store_kernels(g):
                sp.wait_ge(k_ready, g + 1)
                sp.dma_start(bass.AP(kpad.tensor, g * (KG * KPITCH), [[NB, NA], [KPITCH, KG], [1, NB]]),
                             k_rows[:, :, :]).then_inc(k_stored, 16)

            def load_w(n):
                sp.dma_start(w_rows[n], W[n * P:(n + 1) * P, :]).then_inc(w_in[n], 16)

            load_rows(0, 0)
            sp.dma_start(b_rows.rearrange("p e o r -> p e (o r)"),
                         B.rearrange("e (p o) r -> p e (o r)", o=8)).then_inc(b_in, 16)
            for n in range(4):
                load_w(n)
            sp.wait_ge(tables, 1)
            sp.dma_start(d_row[NA - 1:NA, :], D.rearrange("(a h) -> a h", a=1)).then_inc(d_in, 16)
            sp.dma_start(wr_rows[:, :], bass.AP(Wr.tensor, 0, [[P, CH], [LEN, EXPERTS], [1, P]])).then_inc(wr_in, 16)
            sp.wait_ge(consts, 4)
            sp.dma_start(kpad[:, LEN:KPITCH], zeros[:, :]).then_inc(pad_stored, 16)
            sp.wait_ge(px_full, 1)
            load_w(6)
            sp.wait_ge(wt_full, w_tile(0) + 1)
            load_rows(0, 1)
            sp.wait_ge(wt_full, w_tile(1) + 1)
            sp.dma_start(a_rows, A.rearrange("e r d -> (e r) d")).then_inc(a_in, 16)
            sp.wait_ge(b_ready, 1)
            load_w(4)
            sp.wait_ge(wt_full, TILE_B + 1)
            load_w(5)
            sp.dma_start(len_i[:, :], bass.AP(lengths.tensor, 0, [[0, P], [1, SEQS]])).then_inc(small_in, 16)
            for h in range(2):
                sp.dma_start(lang_i[h * SEQS:(h + 1) * SEQS, :],
                             languages.rearrange("(b a) -> b a", a=1)).then_inc(small_in, 16)
            store_kernels(0)
            sp.wait_ge(pad_stored, 16)
            sp.wait_ge(k_stored, 16)
            sp.wait_ge(prm_full, 2)
            for (h, lags), loaded in zip(PARTS, toe_part + toe_in[0:1]):
                n = lags.stop - lags.start
                sp.dma_start(toe[0][:, h, LEN - lags.stop:LEN - lags.start],
                             bass.AP(kpad.tensor, h * KPITCH + LEN - lags.stop, [[1, P], [1, n]])
                             ).then_inc(loaded, 16)
            sp.wait_ge(wt_full, w_tile(5) + 1)
            load_toe(0, 1)
            load_w(7)

            def step(b, m):
                i = BODY * b + m
                sp.wait_ge(px_full, i + 1)
                load_rows(b, m + 2)
                if m + 2 >= BODY:
                    sp.wait_ge(k_stored, 16 * b + 32)
                sp.wait_ge(thi_ready, i + 1)
                sp.wait_ge(tlo_ready, i + 1)
                load_toe(b, m + 2)

            sp.wait_ge(wt_full, w_tile(6) + 1)
            with sp.Fori(0, LAST) as b:
                for m in range(BODY):
                    step(b, m)
                    if m == 1:
                        store_kernels(b + 1)
            for m in range(BODY - 2):
                sp.wait_ge(px_full, BODY * LAST + m + 1)
                load_rows(LAST, m + 2)
                sp.wait_ge(thi_ready, BODY * LAST + m + 1)
                sp.wait_ge(tlo_ready, BODY * LAST + m + 1)
                load_toe(LAST, m + 2)

        @block.gpsimd
        def _(pool):
            nc.gpsimd.memset(ident[:, :], 0.0).then_inc(consts, 1)
            pool.wait_ge(consts, 1)
            nc.gpsimd.affine_select(out=ident[:, :], in_=ident[:, :], compare_op=ALU.not_equal, fill=1.0,
                                    base=0, pattern=[[-1, P]], channel_multiplier=1).then_inc(ident_ready, 1)
            nc.gpsimd.iota(pos[:, 0:NB], [[-1, NB]], base=NB - 1, channel_multiplier=0,
                           allow_small_or_imprecise_dtypes=True).then_inc(consts, 1)
            nc.gpsimd.iota(pos[:, NB:POS], [[-NB, NA]], base=NB * (NA - 1), channel_multiplier=0,
                           allow_small_or_imprecise_dtypes=True).then_inc(consts, 1)
            nc.gpsimd.memset(zeros[:, :], 0.0).then_inc(consts, 1)
            nc.gpsimd.iota(sample_no[:, :], [[P, CH]], base=0, channel_multiplier=1,
                           allow_small_or_imprecise_dtypes=True).then_inc(consts, 1)
            nc.gpsimd.iota(expert_no[:, :], [[1, EXPERTS]], base=0, channel_multiplier=0,
                           allow_small_or_imprecise_dtypes=True).then_inc(consts, 1)

            def sort_b(experts):
                for e in experts:
                    ins = nc.gpsimd.tensor_copy(b_sorted[:, :, e, :], b_rows[:, e, :, :])
                return ins

            pool.wait_ge(b_in, 16)
            sort_b(range(EXPERTS // 2))
            pool.wait_ge(consts, 6)
            pool.wait_ge(prm_ready, 1)

            def products(g):
                heads = bass.ds(g * KG, KG)
                at = pos[:, :].unsqueeze(1).to_broadcast([P, KG, POS])
                nc.gpsimd.tensor_tensor(turn[:, :, :], prm[:, 1, heads].unsqueeze(2).to_broadcast([P, KG, POS]),
                                        at, ALU.mult).then_inc(prod_ready, 1)
                nc.gpsimd.tensor_tensor(mag[:, :, :], prm[:, 0, heads].unsqueeze(2).to_broadcast([P, KG, POS]),
                                        at, ALU.mult).then_inc(prod_ready, 1)

            products(0)
            sort_b(range(EXPERTS // 2, EXPERTS)).then_inc(b_ready, 1)

            def split_rows(s):
                pool.wait_ge(xt_ready, s + 1)
                pool.wait_ge(uhi_ready, s + 1)
                nc.gpsimd.tensor_tensor(u_lo[s], xt[s][:, :, :], u_hi[s].bitcast(F32), ALU.subtract
                                        ).then_inc(ulo_ready, 1)

            split_rows(0)
            split_rows(1)
            with pool.Fori(0, LAST) as b:
                pool.wait_ge(k_full, b + 1)
                products(b + 1)

        @block.scalar
        def _(act):
            def weight(k):
                act.wait_ge(wt_full, k + 1)
                turned, hi = tile_views(k, w_hi, bt_hi)
                nc.scalar.activation(hi, turned, ACT.Copy).then_inc(whi_ready, 1)

            def copy_parameters(k):
                act.wait_ge(prm_full, k // 2 + 1)
                nc.scalar.activation(prm[:, k:k + 2, :],
                                     pg[:, k * HEADS:(k + 2) * HEADS].rearrange("p (k h) -> p k h", k=2), ACT.Copy
                                     ).then_inc(prm_ready, 1)

            def magnitudes(g):
                act.wait_ge(prod_ready, 2 * g + 2)
                nc.scalar.activation(mag[:, :, :], mag[:, :, :], ACT.Exp).then_inc(mag_ready, 1)

            def waves(g):
                act.wait_ge(angle_ready, g + 1)
                nc.scalar.activation(wave[:, :, :], wave[:, :, :], ACT.Sin, scale=-TWO_PI, bias=phase[:, 2:3]
                                     ).then_inc(wave_ready, 1)
                nc.scalar.activation(wave2[:, :, :], wave2[:, :, :], ACT.Sin, scale=-TWO_PI, bias=phase[:, 3:4]
                                     ).then_inc(wave_ready, 1)

            def copy_kernels(g):
                act.wait_ge(k_full, g + 1)
                nc.scalar.activation(k_rows[:, :, :], k_psum, ACT.Copy).then_inc(k_copied, 1)

            def split_rows(b, m, first=False):
                i, s = BODY * b + m, m % 2
                act.wait_ge(px_full, i + 1)
                if not first:
                    act.wait_ge(ylo_ready, i - 1)
                nc.scalar.activation(xt[s][:, :, :], px[:, :, :], ACT.Copy).then_inc(xt_ready, 1)
                if not first:
                    act.wait_ge(conv_done, i - 1)
                nc.scalar.activation(u_hi[s], px[:, :, :], ACT.Copy).then_inc(uhi_ready, 1)

            def split_toe(b, m):
                s = m % 2
                act.wait_ge(toe_in[s], 32 * b + 16 * (m // 2 + 1))
                nc.scalar.activation(t_hi[s][:, :, :], toe_f[s], ACT.Copy).then_inc(thi_ready, 1)

            def copy_far(b, m):
                i = BODY * b + m
                if m > 0:
                    act.wait_ge(merged, i)
                act.wait_ge(conv_done, i + 1)
                nc.scalar.activation(far_sum[:, :, :, :], px_far[:, :, 1, :, :], ACT.Copy).then_inc(far_copied, 1)

            def split_y(b, m):
                s = m % 2
                act.wait_ge(merged, BODY * b + m + 1)
                nc.scalar.activation(y_hi[s][:, :, :], xt[s][:, :, :], ACT.Copy).then_inc(yhi_ready, 1)

            def store_result(i, s, c0, c1):
                for h in range(2):
                    act.dma_start(bass.AP(out.tensor, (2 * i + h) * LEN + c0, [[HEADS * LEN, SEQS], [1, c1 - c0]]),
                                  result[s][h * SEQS:(h + 1) * SEQS, c0:c1]).then_inc(result_dma[s], 16)

            def finish(b, m, kernels=False, last=False):
                i, s = BODY * b + m, m % 2
                act.wait_ge(router, ROUTER * i + 2)
                nc.scalar.activation(ratio[:, :], top[:, 0:1], ACT.Exp, scale=-1.0, bias=top[:, 1:2]
                                     ).then_inc(ratio_ready, 1)
                if kernels:
                    magnitudes(b + 1)
                act.wait_ge(gt_full, i + 1)
                nc.scalar.activation(gt_hi[:, :], pg[:, 0:P], ACT.Copy).then_inc(gthi_ready, 1)
                if kernels:
                    waves(b + 1)
                act.wait_ge(result_dma[s], START + 64 * b + 32 * (m // 2))
                for j, n in enumerate(BANK_ORDER):
                    c0, c1 = BANKS[n][0], min(BANKS[n][1], LEN)
                    act.wait_ge(proj_done, 3 * i + (j + 1))
                    nc.scalar.activation(result[s][:, c0:c1], pm[:, n, 0:c1 - c0], ACT.Copy).then_inc(pm_free, 1)
                    if last and j == 0:
                        act.wait_ge(pm_free, 3 * i + 4)
                        store_result(i, s, c0, c1)
                act.wait_ge(pm_free, 3 * i + 6)
                store_result(i, s, 0, GATE[0] if last else LEN)

            act.sem_inc(pm_free, 3)
            for s in range(2):
                act.sem_inc(result_dma[s], START)
            act.wait_ge(px_full, 1)
            nc.scalar.activation(xt[0][:, :, :], px[:, :, :], ACT.Copy).then_inc(xt_ready, 1)
            copy_parameters(0)
            nc.scalar.activation(tanh_half, dt_re, ACT.Tanh, scale=0.5).then_inc(par_act, 1)
            nc.scalar.activation(sin1, turns, ACT.Sin, scale=TWO_PI).then_inc(par_act, 1)
            nc.scalar.activation(sin_half, turns, ACT.Sin, scale=TWO_PI / 2).then_inc(par_act, 1)
            nc.scalar.activation(u_hi[0], px[:, :, :], ACT.Copy).then_inc(uhi_ready, 1)
            weight(0)
            waves(0)
            nc.scalar.activation(ratio[:, :], phase[:, 0:1], ACT.Exp)
            copy_parameters(2)
            magnitudes(0)
            weight(1)
            weight(2)
            copy_kernels(0)
            for k in range(3, X1_TURN):
                weight(k)
            for n, (h, lags) in enumerate(PARTS):
                act.wait_ge((toe_part + toe_in[0:1])[n], 16)
                nc.scalar.activation(t_hi[0][:, h, lags], toe_f[0][:, h, lags], ACT.Copy
                                     ).then_inc(thi_part if n < 2 else thi_ready, 1)
            split_rows(0, 1, first=True)
            for k in range(X1_TURN, LATE):
                weight(k)
            split_toe(0, 1)
            copy_far(0, 0)
            for k in range(LATE, WTILES):
                weight(k)
            split_y(0, 0)

            def step(b, m, rows_left=True, kernels=True):
                if rows_left:
                    split_rows(b, m + 2)
                    act.wait_ge(conv_done, BODY * b + m + 1)
                    split_toe(b, m + 2)
                copy_far(b, m + 1)
                split_y(b, m + 1)
                if kernels and m == 1:
                    copy_kernels(b + 1)
                finish(b, m, kernels and m == 0)

            with act.Fori(0, LAST) as b:
                for m in range(BODY):
                    step(b, m)
            for m in range(BODY - 1):
                step(LAST, m, rows_left=m < BODY - 2, kernels=False)
            finish(LAST, BODY - 1, last=True)
            act.wait_ge(result_dma[0], START + 16 * PAIRS)
            act.wait_ge(result_dma[1], START + 16 * PAIRS + 32)

        @block.vector
        def _(dve):
            n_par = [0]

            def par_step(ins, behind=0):
                n_par[0] += 1
                ins.then_inc(par_dve, 1)
                dve.wait_ge(par_dve, n_par[0] - behind)

            vec = nc.vector
            vec.memset(d_row[:, :], 0.0)
            vec.memset(phase[0:HEADS, 0:1], 0.25)
            vec.memset(phase[HEADS:P, 0:1], 0.0)
            vec.memset(phase[0:HEADS, 1:2], 0.0)
            vec.memset(phase[HEADS:P, 1:2], 0.25).then_inc(tables, 1)
            dve.wait_ge(tables, 1)
            vec.tensor_scalar(phase[:, 2:4], phase[:, 0:2], TWO_PI, None, ALU.mult).then_inc(tables, 1)

            def angles(g):
                far = turn[:, :, NB:POS]
                dve.wait_ge(prod_ready, 2 * g + 1)
                vec.tensor_scalar(wave[:, :, :], turn[:, :, :], phase[:, 0:1], MAGIC, ALU.add, ALU.add
                                  ).then_inc(angle_step, 1)
                vec.tensor_scalar(wave2[:, :, :], far, phase[:, 1:2], MAGIC, ALU.add, ALU.add).then_inc(angle_step, 1)
                dve.wait_ge(angle_step, 2 * g + 2)
                vec.scalar_tensor_tensor(out=wave[:, :, :], in0=wave[:, :, :], scalar=MAGIC, in1=turn[:, :, :],
                                         op0=ALU.subtract, op1=ALU.subtract)
                vec.scalar_tensor_tensor(out=wave2[:, :, :], in0=wave2[:, :, :], scalar=MAGIC, in1=far,
                                         op0=ALU.subtract, op1=ALU.subtract).then_inc(angle_ready, 1)

            def exact_exp(out, x, n, behind):
                k, q, two_k = ex_k[:, 0:n], ex_q[:, 0:n], ex_2k[:, 0:n]
                yield par_step(vec.tensor_scalar(k, x, 1.0 / math.log(2.0), MAGIC, ALU.mult, ALU.add), behind)
                yield par_step(vec.tensor_scalar(k, k, MAGIC, -126.0, ALU.subtract, ALU.max), behind)
                yield par_step(vec.tensor_scalar(k, k, 127.0, None, ALU.min), behind)
                yield par_step(vec.scalar_tensor_tensor(out=out, in0=k, scalar=-LN2_HI, in1=x,
                                                        op0=ALU.mult, op1=ALU.add), behind)
                yield par_step(vec.scalar_tensor_tensor(out=out, in0=k, scalar=-LN2_LO, in1=out,
                                                        op0=ALU.mult, op1=ALU.add), behind)
                yield par_step(vec.tensor_scalar(q, out, 1.0 / math.factorial(7), None, ALU.mult), behind)
                for m in range(6, 0, -1):
                    yield par_step(vec.scalar_tensor_tensor(out=q, in0=q, scalar=1.0 / math.factorial(m), in1=out,
                                                            op0=ALU.add, op1=ALU.mult), behind)
                yield par_step(vec.tensor_scalar(two_k, k, 127.0, 2.0 ** 23, ALU.add, ALU.mult), behind)
                yield par_step(vec.scalar_tensor_tensor(out=out, in0=q, scalar=1.0, in1=two_k.bitcast(F32),
                                                        op0=ALU.add, op1=ALU.mult), behind)

            dve.wait_ge(logs_in, 32)
            for _ in exact_exp(exps[:, :], logs[:, :], MODES + 1, 0):
                pass
            dve.wait_ge(par_in, 32)
            par_step(vec.tensor_scalar(dt_im, a_im, step_h[:, :], None, ALU.mult), 1)
            par_step(vec.tensor_scalar(dt_re, a_re, step_h[:, :], -1.0, ALU.mult, ALU.mult), 1)
            decay_exp = exact_exp(expo, dt_re, MODES, 1)
            par_step(vec.tensor_scalar(revs, dt_im, 1.0 / (2.0 * math.pi), None, ALU.mult), 1)
            next(decay_exp)
            par_step(vec.tensor_scalar(whole, revs, MAGIC, None, ALU.add), 1)
            next(decay_exp)
            par_step(vec.tensor_scalar(whole, whole, MAGIC, None, ALU.subtract), 1)
            next(decay_exp)
            par_step(vec.tensor_tensor(par[:, 1, halves[0]], revs, whole, ALU.subtract), 1)
            par_step(vec.tensor_tensor(par[:, 1, halves[1]], revs, whole, ALU.subtract), 1)
            par_step(vec.tensor_scalar(par[:, 0, halves[1]], dt_re, 1.0, None, ALU.mult), 0)
            assert n_par[0] == A_STEPS
            next(decay_exp)
            par_step(vec.tensor_tensor(t1, a_re, a_re, ALU.mult), 1)
            next(decay_exp)
            par_step(vec.tensor_tensor(t2, a_im, a_im, ALU.mult), 1)
            next(decay_exp)
            par_step(vec.tensor_tensor(norm, t1, t2, ALU.add), 1)
            next(decay_exp)
            par_step(vec.reciprocal(norm, norm), 1)
            next(decay_exp)
            par_step(vec.scalar_tensor_tensor(out=n_re, in0=a_re, scalar=-2.0, in1=norm, op0=ALU.mult, op1=ALU.mult), 1)
            next(decay_exp)
            par_step(vec.scalar_tensor_tensor(out=n_im, in0=a_im, scalar=-2.0, in1=norm, op0=ALU.mult, op1=ALU.mult), 1)
            next(decay_exp)
            c_re, c_im = c_in[:, :, 0], c_in[:, :, 1]
            par_step(vec.tensor_tensor(t1, c_re, n_re, ALU.mult), 1)
            next(decay_exp)
            par_step(vec.tensor_tensor(t2, c_im, n_im, ALU.mult), 1)
            next(decay_exp)
            par_step(vec.tensor_tensor(t3, c_re, n_im, ALU.mult), 1)
            next(decay_exp)
            par_step(vec.tensor_tensor(t4, c_im, n_re, ALU.mult), 1)
            next(decay_exp)
            par_step(vec.tensor_tensor(g_re, t1, t2, ALU.subtract), 1)
            par_step(vec.tensor_tensor(g_im, t3, t4, ALU.add), 1)
            angles(0)
            dve.wait_ge(par_act, 3)
            par_step(vec.scalar_tensor_tensor(out=em1, in0=expo, scalar=1.0, in1=tanh_half, op0=ALU.add, op1=ALU.mult), 1)
            par_step(vec.scalar_tensor_tensor(out=cos1, in0=sin_half, scalar=-2.0, in1=sin_half,
                                              op0=ALU.mult, op1=ALU.mult), 0)
            par_step(vec.scalar_tensor_tensor(out=t1, in0=cos1, scalar=1.0, in1=em1, op0=ALU.add, op1=ALU.mult), 1)
            par_step(vec.tensor_tensor(e_im, expo, sin1, ALU.mult), 1)
            par_step(vec.tensor_tensor(e_re, t1, cos1, ALU.add), 1)
            par_step(vec.tensor_tensor(t2, g_im, e_im, ALU.mult), 1)
            par_step(vec.tensor_tensor(t1, g_re, e_re, ALU.mult), 1)
            par_step(vec.tensor_tensor(t3, g_re, e_im, ALU.mult), 1)
            par_step(vec.tensor_tensor(t4, g_im, e_re, ALU.mult), 1)
            par_step(vec.tensor_tensor(par[:, 2, halves[0]], t1, t2, ALU.subtract), 1)
            par_step(vec.tensor_tensor(par[:, 2, halves[1]], t2, t1, ALU.subtract), 1)
            for half in halves:
                par_step(vec.scalar_tensor_tensor(out=par[:, 3, half], in0=t3, scalar=-1.0, in1=t4,
                                                  op0=ALU.mult, op1=ALU.subtract), 1)
            assert n_par[0] == PAR_STEPS

            def low_weight(k):
                dve.wait_ge(whi_ready, k + 1)
                turned, hi = tile_views(k, w_hi, bt_hi)
                vec.tensor_tensor(tile_views(k, w_lo, bt_lo)[1], turned, hi.bitcast(F32), ALU.subtract
                                  ).then_inc(wlo_ready, 1)

            def factors(g):
                heads = bass.ds(g * KG, KG)
                far = wave[:, :, NB:POS]
                dve.wait_ge(wave_ready, 2 * g + 2)
                vec.tensor_tensor(far, far, prm[:, 2, heads].unsqueeze(2).to_broadcast([P, KG, NA]), ALU.mult
                                  ).then_inc(fac_step, 1)
                vec.tensor_tensor(wave2[:, :, :], wave2[:, :, :],
                                  prm[:, 3, heads].unsqueeze(2).to_broadcast([P, KG, NA]), ALU.mult
                                  ).then_inc(fac_step, 1)
                dve.wait_ge(fac_step, 3 * g + 2)
                vec.tensor_tensor(far, far, wave2[:, :, :], ALU.add).then_inc(fac_step, 1)
                dve.wait_ge(fac_step, 3 * g + 3)
                dve.wait_ge(mag_ready, g + 1)
                vec.tensor_tensor(wave[:, :, :], wave[:, :, :], mag[:, :, :], ALU.mult).then_inc(fac_ready, 1)

            def first_samples(g):
                dve.wait_ge(k_copied, g + 1)
                at0 = k_rows[:, :, NB - 1:NB].rearrange("p h q -> p (h q)")
                vec.tensor_tensor(at0, at0, d_one[:, bass.ds(g * KG, KG)], ALU.add).then_inc(k_ready, 1)

            def split_rows(b, m):
                i, s = BODY * b + m, m % 2
                dve.wait_ge(xt_ready, i + 1)
                dve.wait_ge(uhi_ready, i + 1)
                dve.wait_ge(conv_done, i - 1)
                vec.tensor_tensor(u_lo[s], xt[s][:, :, :], u_hi[s].bitcast(F32), ALU.subtract
                                  ).then_inc(ulo_ready, 1)

            def split_toe(b, m):
                s = m % 2
                dve.wait_ge(thi_ready, BODY * b + m + 1)
                vec.tensor_tensor(t_lo[s][:, :, :], toe_f[s], t_hi[s][:, :, :].bitcast(F32), ALU.subtract
                                  ).then_inc(tlo_ready, 1)

            def hold():
                vec.tensor_copy(held[:, :], lang_f[:, :])

            def merge(b, m, first=False):
                i, s = BODY * b + m, m % 2
                dve.wait_ge(ulo_ready, i + 1)
                dve.wait_ge(conv_done, i + 1)
                dve.wait_ge(far_copied, i + 1)
                vec.tensor_tensor(far_sum[:, :, :, :], far_sum[:, :, :, :], px_far[:, :, 0, :, :], ALU.add
                                  ).then_inc(far_added, 1)
                dve.wait_ge(far_added, 2 * i + 1)
                vec.tensor_tensor(pc_far, pc_far, far_sum[:, :, :, :], ALU.add).then_inc(far_added, 1)
                dve.wait_ge(far_added, 2 * i + 2)
                hold()
                for h in range(2):
                    ins = vec.copy_predicated(xt[s][:, :, h * SEQS:(h + 1) * SEQS], valid[:, :, :], pc[:, h, :, :])
                ins.then_inc(merged, 1)
                if first:
                    for k in range(LATE, WTILES):
                        low_weight(k)
                dve.wait_ge(yhi_ready, i + 1)
                vec.tensor_tensor(y_lo[s][:, :, :], xt[s][:, :, :], y_hi[s][:, :, :].bitcast(F32), ALU.subtract
                                  ).then_inc(ylo_ready, 1)

            def route(b, m):
                i = BODY * b + m
                gate = pm[:, 2, :]
                base = ROUTER * i
                dve.wait_ge(gate_done, i + 1)
                vec.tensor_tensor(logits[:, :], gate[:, L0:L0 + EXPERTS], bias[:, :], ALU.add).then_inc(router, 1)
                dve.wait_ge(router, base + 1)
                hold()
                vec.max(top[:, :], logits[:, :]).then_inc(router, 1)
                dve.wait_ge(router, base + 2)
                hold()
                vec.max_index(top_at[:, :], top[:, :], logits[:, :]).then_inc(router, 1)
                dve.wait_ge(router, base + 3)
                vec.tensor_copy(top_no[:, :], top_at[:, 0:2]).then_inc(router, 1)
                dve.wait_ge(ratio_ready, i + 1)
                vec.tensor_scalar(half_sum[:, :], ratio[:, :], 1.0 / SCALING, 1.0 / SCALING, ALU.mult, ALU.add
                                  ).then_inc(router, 1)
                dve.wait_ge(router, base + 5)
                vec.reciprocal(weight[:, 0:1], half_sum[:, :]).then_inc(router, 1)
                dve.wait_ge(router, base + 6)
                vec.tensor_tensor(weight[:, 1:2], weight[:, 0:1], ratio[:, :], ALU.mult).then_inc(router, 1)
                vec.tensor_scalar(gate1[:, :], expert_no[:, :], top_no[:, 0:1], weight[:, 0:1],
                                  ALU.is_equal, ALU.mult)
                dve.wait_ge(router, base + 7)
                vec.tensor_scalar(gate2[:, :], expert_no[:, :], top_no[:, 1:2], weight[:, 1:2],
                                  ALU.is_equal, ALU.mult).then_inc(router, 1)
                dve.wait_ge(router, base + 8)
                vec.tensor_tensor(gates[:, :], gate1[:, :], gate2[:, :], ALU.add).then_inc(router, 1)
                dve.wait_ge(router, base + 9)
                vec.tensor_tensor(gated[:, :, :], gate[:, H0:L0].rearrange("p (e r) -> p e r", e=EXPERTS),
                                  gates[:, :].unsqueeze(2).to_broadcast([P, EXPERTS, RANK]), ALU.mult
                                  ).then_inc(gated_ready, 1)
                dve.wait_ge(gthi_ready, i + 1)
                vec.tensor_tensor(gt_lo[:, :], pg[:, 0:P], gt_hi[:, :].bitcast(F32), ALU.subtract
                                  ).then_inc(gtlo_ready, 1)

            dve.wait_ge(d_in, 16)
            dve.wait_ge(ident_ready, 1)
            vec.tensor_scalar(d_one[:, :], d_row[:, :], ident[0:NA, NA - 1:NA], None, ALU.add).then_inc(tables, 1)
            dve.wait_ge(prm_ready, 2)
            factors(0)
            for k in range(2):
                low_weight(k)
            dve.wait_ge(tables, 3)
            first_samples(0)
            for k in range(2, 4):
                low_weight(k)
            dve.wait_ge(small_in, 48)
            dve.wait_ge(consts, 6)
            vec.tensor_copy(len_f[:, :], len_i[:, :]).then_inc(masks, 1)
            vec.tensor_copy(lang_f[:, :], lang_i[:, :]).then_inc(masks, 1)
            dve.wait_ge(masks, 2)
            vec.tensor_tensor(valid[:, :, :], sample_no[:, :].unsqueeze(2).to_broadcast([P, CH, SEQS]),
                              len_f[:, :].unsqueeze(1).to_broadcast([P, CH, SEQS]), ALU.is_lt).then_inc(masks, 1)
            vec.tensor_scalar(bias[:, :], expert_no[:, :], lang_f[:, :], LANG_BIAS, ALU.is_equal, ALU.mult
                              ).then_inc(masks, 1)
            for k in range(4, X1_TURN):
                low_weight(k)
            for n, (h, lags) in enumerate(PARTS):
                dve.wait_ge(thi_part if n < 2 else thi_ready, n % 2 + 1)
                vec.tensor_tensor(t_lo[0][:, h, lags], toe_f[0][:, h, lags], t_hi[0][:, h, lags].bitcast(F32),
                                  ALU.subtract).then_inc(tlo_part if n < 2 else tlo_ready, 1)
            for k in range(X1_TURN, LATE):
                low_weight(k)
            split_toe(0, 1)
            dve.wait_ge(masks, 4)
            merge(0, 0, first=True)

            def step(b, m, rows_left=True, kernels=True):
                if kernels and m == 0:
                    angles(b + 1)
                if kernels and m == 1:
                    factors(b + 1)
                if rows_left:
                    split_rows(b, m + 2)
                merge(b, m + 1)
                if kernels and m == 1:
                    first_samples(b + 1)
                route(b, m)
                if rows_left:
                    split_toe(b, m + 2)

            with dve.Fori(0, LAST) as b:
                for m in range(BODY):
                    step(b, m)
            for m in range(BODY - 1):
                step(LAST, m, rows_left=m < BODY - 2, kernels=False)
            route(LAST, BODY - 1)

        @block.tensor
        def _(pe):
            pe.wait_ge(ident_ready, 1)

            def turn_weight(k):
                what, place, at = TILE[k]
                loaded, staged = {W_: (w_in[at.start // P], w_rows[at.start // P]) if what == W_ else None,
                                  A_: (a_in, a_rows), WR_: (wr_in, wr_rows), B_: (b_ready, b_sorted)}[what]
                pe.wait_ge(loaded, 1 if what == B_ else 16)
                before = [j for j in range(k) if TILE[j][1] is place]
                if before:
                    pe.wait_ge(wlo_ready, before[-1] + 1)
                if place is in_pg and what == W_:
                    pe.wait_ge(k_copied, 1)
                if place is in_px:
                    pe.wait_ge(uhi_ready, 1)
                if what == WR_:
                    place = place.rearrange("p c o -> p (c o)")
                    nc.tensor.transpose(place[:, 0:CH * EXPERTS], staged[:, :], ident[0:CH * EXPERTS, 0:CH * EXPERTS]
                                        ).then_inc(wt_full, 1)
                    return
                for c in range(CH):
                    chunk = (staged[:, c, :, :].rearrange("p e r -> p (e r)") if what == B_
                             else staged[:, c * P:(c + 1) * P])
                    ins = nc.tensor.matmul(place[:, c, :], chunk, ident[:, :], is_transpose=True,
                                           start=c % 4 == 0, stop=True, skip_group_check=True)
                if what == W_:
                    ins = nc.tensor.matmul(place[:, at.start // P, :], ident[:, :], ident[:, :], start=False, stop=True,
                                           skip_group_check=True)
                ins.then_inc(wt_full, 1)

            def turn_parameters(k):
                for n in (k, k + 1):
                    ins = nc.tensor.transpose(pg[:, n * HEADS:(n + 1) * HEADS], par[:, n, :],
                                              ident[0:HEADS, 0:HEADS])
                ins.then_inc(prm_full, 1)

            def make_kernels(g):
                pe.wait_ge(fac_ready, g + 1)
                for h in range(KG):
                    ins = nc.tensor.matmul(k_psum[:, h, :], wave[:, h, NB:POS], wave[:, h, 0:NB],
                                           start=True, stop=True)
                ins.then_inc(k_full, 1)

            def turn_rows(b, m, first=False):
                i, s = BODY * b + m, m % 2
                pe.wait_ge(rows_in[s], 64 * b + 32 * (m // 2 + 1))
                if not first:
                    pe.wait_ge(uhi_ready, i)
                    pe.wait_ge(merged, i - 1)
                for c in range(CH):
                    ins = nc.tensor.transpose(px[:, c, :], rows[s][:, c * P:(c + 1) * P], ident[:, :])
                ins.then_inc(px_full, 1)

            def convolve(b, m, first=False, turned=True):
                i, s = BODY * b + m, m % 2
                pe.wait_ge(uhi_ready, i + 1)
                pe.wait_ge(ulo_ready, i + 1)
                if first:
                    pe.wait_ge(thi_part, 1)
                    pe.wait_ge(tlo_part, 1)
                    pe.wait_ge(wlo_ready, w_tile(5) + 1)
                else:
                    pe.wait_ge(thi_ready, i + 1)
                    pe.wait_ge(tlo_ready, i + 1)
                    pe.wait_ge(merged, i)
                for h in range(2):
                    if first and h == 1:
                        pe.wait_ge(thi_ready, 1)
                        pe.wait_ge(tlo_ready, 1)
                    tok = slice(h * SEQS, (h + 1) * SEQS)
                    for d in range(CH):
                        if first and h == 0 and d == CH // 2:
                            pe.wait_ge(thi_part, 2)
                            pe.wait_ge(tlo_part, 2)
                        n = CH - d
                        near = d < FAR
                        for t, v in ((t_hi, u_hi), (t_hi, u_lo), (t_lo, u_hi)) if near else ((t_lo, u_hi),):
                            ins = nc.tensor.matmul(pc[:, h, d:CH, :], t[s][:, h, d * P:(d + 1) * P], v[s][:, 0:n, tok],
                                                   start=(d == 0 and v is u_hi and t is t_hi), stop=d == CH - 1)
                if turned:
                    pe.wait_ge(uhi_ready, i + 2)
                for h in range(2):
                    for d in range(FAR, CH):
                        ins = nc.tensor.matmul(px_far[:, h, :, d - FAR:, :], t_hi[s][:, h, d * P:(d + 1) * P],
                                               u[s][:, :, 0:CH - d, h * SEQS:(h + 1) * SEQS],
                                               start=d == FAR, stop=d == CH - 1)
                ins.then_inc(conv_done, 1)

            def add_lora(n):
                c0, c1 = BANKS[n][0], min(BANKS[n][1], LEN)
                for g, w in ((gt_hi, bt_hi), (gt_lo, bt_hi), (gt_hi, bt_lo)):
                    ins = nc.tensor.matmul(pm[:, n, 0:c1 - c0], g[:, :], w[:, c0:c1], start=False,
                                           stop=w is bt_lo, skip_group_check=True)
                ins.then_inc(proj_done, 1)

            def project(b, m):
                i, s = BODY * b + m, m % 2
                pe.wait_ge(yhi_ready, i + 1)
                pe.wait_ge(ylo_ready, i + 1)
                for j, n in enumerate(BANK_ORDER):
                    c0, c1 = BANKS[n]
                    pe.wait_ge(pm_free, 3 * i + (j + 1))
                    for c in range(CH):
                        if n == 1 and c == CH - 1:
                            pe.wait_ge(gthi_ready, i + 1)
                            pe.wait_ge(gtlo_ready, i + 1)
                            add_lora(BANK_ORDER[0])
                            add_lora(BANK_ORDER[1])
                        if n == 1 and c == CH // 2:
                            pe.wait_ge(gated_ready, i + 1)
                            if m == 1:
                                pe.wait_ge(k_copied, b + 2 if b is not LAST else KGROUPS)
                            nc.tensor.transpose(pg[:, 0:P], gated[:, :, :].rearrange("p e r -> p (e r)"), ident[:, :]
                                                ).then_inc(gt_full, 1)
                        for y, w in ((y_hi, w_hi), (y_lo, w_hi), (y_hi, w_lo)):
                            ins = nc.tensor.matmul(pm[:, n, 0:c1 - c0], y[s][:, c, :], w[:, c, c0:c1],
                                                   start=(c == 0 and y is y_hi and w is w_hi),
                                                   stop=(c == CH - 1 and w is w_lo), skip_group_check=True)
                    if n == 2:
                        ins.then_inc(gate_done, 1)
                add_lora(BANK_ORDER[2])

            turn_rows(0, 0, first=True)
            pe.wait_ge(par_dve, A_STEPS)
            turn_parameters(0)
            for k in range(2):
                turn_weight(k)
            pe.wait_ge(par_dve, PAR_STEPS)
            turn_parameters(2)
            turn_weight(2)
            pe.wait_ge(prm_ready, 2)
            make_kernels(0)
            for k in range(3, X1_TURN):
                turn_weight(k)
            pe.wait_ge(wlo_ready, TILE_B + 1)
            pe.wait_ge(uhi_ready, 1)
            turn_rows(0, 1, first=True)
            for k in range(X1_TURN, LATE):
                turn_weight(k)
            convolve(0, 0, first=True)
            for k in range(LATE, WTILES):
                turn_weight(k)

            def step(b, m, rows_left=True, kernels=True):
                if rows_left:
                    turn_rows(b, m + 2)
                convolve(b, m + 1, turned=rows_left)
                if kernels and m == 1:
                    make_kernels(b + 1)
                project(b, m)

            with pe.Fori(0, LAST) as b:
                for m in range(BODY):
                    step(b, m)
            for m in range(BODY - 1):
                step(LAST, m, rows_left=m < BODY - 2, kernels=False)
            project(LAST, BODY - 1)


_INS = ["x", "itok_B_8_3872", "itok_B_0_7", "L0_cond_log_dt", "L0_cond_C", "L0_cond_log_A_real", "L0_cond_A_imag",
        "L0_cond_D", "L1_cond_W", "L1_cond_Wr", "L1_cond_A", "L1_cond_B"]


def kernel(**inputs):
    import numpy as _np
    import concourse.bacc as _bacc
    from concourse import mybir as _mybir
    from concourse.bass_utils import run_bass_kernel_spmd as _run

    nc = _bacc.Bacc("TRN2", target_bir_lowering=False, num_devices=1)
    arrays, args = {}, []
    for name in _INS:
        a = _np.ascontiguousarray(inputs[name])
        arrays[f"in_{name}"] = a
        args.append(nc.dram_tensor(f"in_{name}", a.shape, _mybir.dt.from_np(a.dtype), kind="ExternalInput").ap())
    args.append(nc.dram_tensor("out_0", (SEQS, HEADS, LEN), _mybir.dt.float32, kind="ExternalOutput").ap())
    cond_resid_kernel(nc, *args)
    r = _run(nc, [arrays], core_ids=[0])
    return r.results[0]["out_0"]
```
